# Optimizing a Trainium2 kernel written in Bass

```python
import numpy as np
import jax
import jax.numpy as jnp

def _softmax(x, axis=-1):
    return jax.nn.softmax(x, axis=axis)

def _gelu(x):
    return jax.nn.gelu(x, approximate=True)

def _silu(x):
    return jax.nn.silu(x)

def _sigmoid(x):
    return jax.nn.sigmoid(x)

def _layernorm(x, axis=-1, eps=1e-05):
    m = jnp.mean(x, axis=axis, keepdims=True)
    v = jnp.var(x, axis=axis, keepdims=True)
    return (x - m) / jnp.sqrt(v + eps)

def _scatter_add(tgt, idx, src, axis=0):
    return tgt.at[idx].add(src)

def _segment_sum(src, seg, n):
    return jax.ops.segment_sum(src, seg, n)
kernel_name = 'mk_adaln_d1_jaxref_r8_1d6a4a'

def setup_inputs(seed: int=0):
    np.random.seed(seed)
    _w = jnp.asarray

    def _L0_attn_setup():
        import jax, jax.numpy as jnp
        import numpy as np
        B, S, H = (2, 256, 256)
        NH, HD = (16, H // 16)
        WINDOW = 128
        THETA = 10000.0
        EPS = 1e-06

        def rmsnorm(x, w):
            var = jnp.mean(jnp.square(x), axis=-1, keepdims=True)
            return x * jax.lax.rsqrt(var + EPS) * w

        def rope(x, cos, sin):
            d2 = x.shape[-1] // 2
            x1, x2 = (x[..., :d2], x[..., d2:])
            c = cos[None, :, None, :]
            s = sin[None, :, None, :]
            return jnp.concatenate([x1 * c - x2 * s, x2 * c + x1 * s], axis=-1)
        key = jax.random.key(seed)
        k1, k2, k3 = jax.random.split(key, 3)
        sc = 1.0 / np.sqrt(H)
        return {'hidden_states': jax.random.normal(k1, (B, S, H), dtype=jnp.float32), 'Wqkv': jax.random.normal(k2, (H, 3 * H), dtype=jnp.float32) * sc, 'q_norm_w': jnp.ones((H,), dtype=jnp.float32), 'k_norm_w': jnp.ones((H,), dtype=jnp.float32), 'Wo': jax.random.normal(k3, (H, H), dtype=jnp.float32) * sc}
    _L0_attn_in = _L0_attn_setup()

    def _L0_ffn_setup():
        import jax, jax.numpy as jnp
        import numpy as np
        B, S, D, R, E = (4, 256, 256, 64, 8)
        SCALING = 64.0 / 16.0
        key = jax.random.key(seed)
        k1, k2, k3, k4 = jax.random.split(key, 4)
        x = jax.random.normal(k1, (B, S, D), dtype=jnp.float32)
        A = jax.random.normal(k2, (E, R, D), dtype=jnp.float32) * 0.02
        Bw = jax.random.normal(k3, (E, D, R), dtype=jnp.float32) * 0.02
        Wg = jax.random.normal(k4, (E, D), dtype=jnp.float32) * 0.02
        return {'x': x, 'A': A, 'Bw': Bw, 'Wg': Wg}
    _L0_ffn_in = _L0_ffn_setup()
    _L0_c = _w((lambda *s: np.random.randn(*s).astype(np.float32) * 0.05)(4, 256))
    _L0_wmod = _w((lambda *s: np.random.randn(*s).astype(np.float32) * 0.05)(256, 6 * 256) * 256 ** (-0.5))
    _d = {'L0_attn_hidden_states': _L0_attn_in['hidden_states'], 'L0_attn_Wqkv': _L0_attn_in['Wqkv'], 'L0_attn_q_norm_w': _L0_attn_in['q_norm_w'], 'L0_attn_k_norm_w': _L0_attn_in['k_norm_w'], 'L0_attn_Wo': _L0_attn_in['Wo'], 'L0_ffn_A': _L0_ffn_in['A'], 'L0_ffn_Bw': _L0_ffn_in['Bw'], 'L0_ffn_Wg': _L0_ffn_in['Wg'], 'L0_c': _L0_c, 'L0_wmod': _L0_wmod}
    _x0 = _d['L0_attn_hidden_states']
    _d['L0_attn_hidden_states'] = jax.random.normal(jax.random.fold_in(jax.random.key(seed), 1), (4, 512, 256), dtype=_x0.dtype)
    del _x0
    return _d

def reference(L0_attn_hidden_states, L0_attn_Wqkv, L0_attn_q_norm_w, L0_attn_k_norm_w, L0_attn_Wo, L0_ffn_A, L0_ffn_Bw, L0_ffn_Wg, L0_c, L0_wmod):

    def _L0_attn_ref(hidden_states, Wqkv, q_norm_w, k_norm_w, Wo):
        import jax, jax.numpy as jnp
        import numpy as np
        B, S, H = (2, 256, 256)
        NH, HD = (16, H // 16)
        WINDOW = 128
        THETA = 10000.0
        EPS = 1e-06

        def rmsnorm(x, w):
            var = jnp.mean(jnp.square(x), axis=-1, keepdims=True)
            return x * jax.lax.rsqrt(var + EPS) * w

        def rope(x, cos, sin):
            d2 = x.shape[-1] // 2
            x1, x2 = (x[..., :d2], x[..., d2:])
            c = cos[None, :, None, :]
            s = sin[None, :, None, :]
            return jnp.concatenate([x1 * c - x2 * s, x2 * c + x1 * s], axis=-1)
        b, s, h = hidden_states.shape
        qkv = hidden_states @ Wqkv
        q, k, v = jnp.split(qkv, 3, axis=-1)
        q = rmsnorm(q, q_norm_w)
        k = rmsnorm(k, k_norm_w)
        q = q.reshape(b, s, NH, HD)
        k = k.reshape(b, s, NH, HD)
        v = v.reshape(b, s, NH, HD)
        inv_freq = 1.0 / THETA ** (jnp.arange(0, HD, 2, dtype=jnp.float32) / HD)
        freqs = jnp.arange(s, dtype=jnp.float32)[:, None] * inv_freq[None, :]
        cos, sin = (jnp.cos(freqs), jnp.sin(freqs))
        q = rope(q, cos, sin)
        k = rope(k, cos, sin)
        q_idx = jnp.arange(s)[:, None]
        k_idx = jnp.arange(s)[None, :]
        mask = (q_idx >= k_idx) & (q_idx - k_idx <= WINDOW - 1)
        scale = 1.0 / np.sqrt(HD)
        scores = jnp.einsum('bqhd,bkhd->bhqk', q, k) * scale
        scores = jnp.where(mask[None, None, :, :], scores, jnp.float32(-jnp.inf))
        probs = jax.nn.softmax(scores, axis=-1)
        o = jnp.einsum('bhqk,bkhd->bqhd', probs, v).reshape(b, s, h)
        return o @ Wo

    def _L0_ffn_ref(x, A, Bw, Wg):
        import jax, jax.numpy as jnp
        import numpy as np
        B, S, D, R, E = (4, 256, 256, 64, 8)
        SCALING = 64.0 / 16.0
        bsz, seq_len, dim = x.shape
        xf = x.reshape(-1, dim)
        logits = jnp.einsum('nd,ed->ne', xf, Wg)
        prob = jax.nn.softmax(logits, axis=-1)
        gate = jnp.argmax(prob, axis=-1)
        prob_sel = jnp.take_along_axis(prob, gate[:, None], axis=1)
        mask = jax.nn.one_hot(gate, E, dtype=xf.dtype)
        h = jnp.einsum('nd,erd->ner', xf, A)
        h = h * mask[:, :, None]
        y = jnp.einsum('ner,eor->no', h, Bw)
        y = y * SCALING * prob_sel
        return y.reshape(bsz, seq_len, -1)
    x = L0_attn_hidden_states
    mod = (_silu(L0_c) @ L0_wmod).reshape(L0_c.shape[0], 6, 1, -1)
    sa, ca, ga, sb, cb, gb = (mod[:, 0], mod[:, 1], mod[:, 2], mod[:, 3], mod[:, 4], mod[:, 5])
    ga = (2 * (ga >= 0) - 1) * jnp.maximum(jnp.abs(ga), 0.25)
    gb = (2 * (gb >= 0) - 1) * jnp.maximum(jnp.abs(gb), 0.25)
    h = _layernorm(x, axis=-1) * (1 + ca) + sa
    x = x + ga * _L0_attn_ref(h, L0_attn_Wqkv, L0_attn_q_norm_w, L0_attn_k_norm_w, L0_attn_Wo)
    h = _layernorm(x, axis=-1) * (1 + cb) + sb
    x = x + gb * _L0_ffn_ref(h, L0_ffn_A, L0_ffn_Bw, L0_ffn_Wg)
    return x

_drawn_inputs = setup_inputs


def setup_inputs(seed=0):
    import zlib

    import numpy as np

    out = dict(_drawn_inputs(seed))
    spreads = {'L0_attn_q_norm_w': (1.0, 0.6), 'L0_attn_k_norm_w': (1.0, 0.6)}
    factors = {'L0_ffn_A': 5.655, 'L0_ffn_Bw': 5.516, 'L0_ffn_Wg': 5.942}
    for name, (base, spread) in spreads.items():
        noise = np.random.default_rng([zlib.crc32(name.encode()), seed]).standard_normal(out[name].shape)
        drawn = base * np.exp(spread * noise) if base else spread * noise
        out[name] = jnp.asarray(drawn.astype(out[name].dtype))
    for name, factor in factors.items():
        out[name] = (out[name] * factor).astype(out[name].dtype)
    return out
```

```python
from contextlib import ExitStack

import numpy as np
import concourse.bass as bass
from concourse import mybir

F32 = mybir.dt.float32
F32R = mybir.dt.float32r
BF16 = mybir.dt.bfloat16
U8 = mybir.dt.uint8
ALU = mybir.AluOpType
ACT = mybir.ActivationFunctionType
AX = mybir.AxisListType

P = 128
BATCH, SEQ, D = 4, 512, 256
NH, HD = 16, 16
HALF = HD // 2
JT = SEQ // P
TILES = BATCH * JT
DC = D // P
EXPERTS, RANK = 8, 64
ER = EXPERTS * RANK
EC = ER // P
CH = 4
NC = NH // CH
NG = NH // 2
VW = HD + 1
NEG = -1.0e30
EPS_RMS, EPS_LN = 1e-6, 1e-5
SCALING = 64.0 / 16.0

S_BANK = (0, 2)
PT_BANK = (4, 5)
W6, W7 = 6, 7


class At:

    def __init__(self, seq, k):
        self.seq, self.k = seq, k
        self.peeled = isinstance(seq, int)
        self.j = k % JT
        self.index = seq * JT + k
        self.sequence = seq + k // JT

    def count(self, per=1, extra=0):
        least = (self.seq if self.peeled else 1) * JT * per + self.k * per + extra
        if self.peeled:
            return least if least > 0 else None
        assert least > 0
        return self.seq * (JT * per) + (self.k * per + extra)


def wait(eng, sem, value):
    if value is not None:
        eng.wait_ge(sem, value)


def wait_alone(eng, sem, value, target, done):
    if value is None or isinstance(value, int):
        wait(eng, sem, value)
    else:
        eng.reg_mov(target, value)
        eng.wait_ge(done, 1)
        eng.wait_ge(sem, target)


STAGES = (("L", -1), ("P", 0), ("T", 1), ("F", 2), ("G", 3))


def run_slots(eng, slot):
    def live(s):
        return {n for n, lag in STAGES if 0 <= s - lag < TILES}
    for r in range(JT):
        slot(0, r, live(r))
    with eng.Fori(1, BATCH - 1) as seq:
        for r in range(JT):
            slot(seq, r, live(JT + r))
    for r in range(JT + 3):
        slot(BATCH - 1, r, live(TILES - JT + r))


def build(nc, x, c_t, wmod, wqkv, qw, kw, wo, up_t, down, gate_t, trig, out):
    x_t = x.rearrange("(n p) d -> n p d", p=P)
    out_t = out.rearrange("(n p) d -> n p d", p=P)
    with ExitStack() as ctx:
        def sb(name, shape, dt=F32):
            return ctx.enter_context(nc.sbuf_tensor(name, shape, dt))

        def sem(name):
            return ctx.enter_context(nc.semaphore(name))

        ps = ctx.enter_context(nc.psum_tensor("ps", [P, 8, 512], F32))

        wqkv_s = sb("wqkv_s", [P, DC, 3 * D])
        wo_s = sb("wo_s", [P, DC, D])
        wmod_s = sb("wmod_s", [P, DC, 6 * D])
        up_s = sb("up_s", [P, DC, ER])
        down_s = sb("down_s", [P, EC, D])
        gate_s = sb("gate_s", [P, DC, EXPERTS])
        c_s = sb("c_s", [P, DC, BATCH])
        trig_s = sb("trig_s", [P, JT, 2, 2, HD])
        normw = sb("normw", [P, 2, D])
        ident = sb("ident", [P, P])
        ident_b = sb("ident_b", [P, P], BF16)
        ones_f = sb("ones_f", [P, P])
        take_prev = sb("take_prev", [P, P], U8)
        take_f = sb("take_f", [P, P])
        neg_s = sb("neg_s", [P, P])
        pow_s = sb("pow_s", [P, 2])
        first_s = sb("first_s", [P, EXPERTS])
        cosw = sb("cosw", [P, JT, 2, D])
        sinw = sb("sinw", [P, JT, 2, D])
        ec = sb("ec", [P, DC, BATCH])
        ec1 = sb("ec1", [P, DC, BATCH])
        sig = sb("sig", [P, DC, BATCH])
        silu = sb("silu", [P, DC, BATCH])
        silu_rows = sb("silu_rows", [P, DC, BATCH, P])
        mod_s = sb("mod_s", [P, 4, DC, BATCH])
        gates = sb("gates", [P, BATCH, 2, D])
        gtmp = sb("gtmp", [P, 2 * D])
        gsgn = sb("gsgn", [P, 2 * D])
        xs = sb("xs", [P, JT, D])
        st1 = sb("st1", [P, 6])
        mv1 = sb("mv1", [P, 2])
        ve1 = sb("ve1", [P, 1])
        rs1 = sb("rs1", [P, 1])
        xn = sb("xn", [P, D])
        hT = sb("hT", [P, DC, P])
        qk = sb("qk", [P, 2, D])
        sq = sb("sq", [P, D])
        ssq = sb("ssq", [P, 2])
        ssqe = sb("ssqe", [P, 2])
        rqk = sb("rqk", [P, 2])
        t1 = sb("t1", [P, 2, D])
        t2 = sb("t2", [P, 2, D])
        rot = sb("rot", [P, 2, D])
        rr = sb("rr", [P, 2, D])
        hilo = sb("hilo", [P, 2, NH, 4, HD], F32R)
        qT = sb("qT", [P, NG, P], F32R)
        kT = sb("kT", [P, NG, 2, JT, P], F32R)
        v_s = sb("v_s", [P, JT, NH, VW])
        negm = sb("negm", [P, 2, CH])
        shifted = sb("shifted", [P, 2, CH, P])
        expT = sb("expT", [P, 2, CH, P])
        own_p = sb("own_p", [P, 2, CH, P])
        prev_p = sb("prev_p", [P, 2, CH, P])
        oT = sb("oT", [P, NC, P])
        rden = sb("rden", [P, NH])
        on = sb("on", [P, NH, HD])
        onT = sb("onT", [P, DC, P])
        yg = sb("yg", [P, D])
        x1 = sb("x1", [P, 2, D])
        st2 = sb("st2", [P, 6])
        mv2 = sb("mv2", [P, 2])
        ve2 = sb("ve2", [P, 1])
        rs2 = sb("rs2", [P, 1])
        xn2 = sb("xn2", [P, D])
        h2T = sb("h2T", [P, DC, P])
        lgs = sb("lgs", [P, EXPERTS])
        nmx = sb("nmx", [P, 1])
        ge = sb("ge", [P, EXPERTS])
        score = sb("score", [P, EXPERTS])
        best = sb("best", [P, 1])
        onehot = sb("onehot", [P, EXPERTS, RANK], BF16)
        lexp = sb("lexp", [P, EXPERTS])
        lsum = sb("lsum", [P, 1])
        psel = sb("psel", [P, 1])
        maskT = sb("maskT", [P, EC, P], BF16)
        hm = sb("hm", [P, EC, P])
        z = sb("z", [P, D])
        obuf = sb("obuf", [P, 2, D])

        ld_c, ld_mod, ld_trig, ld_w = sem("ld_c"), sem("ld_mod"), sem("ld_trig"), sem("ld_w")
        ld_x = [sem(f"ld_x{j}") for j in range(JT)]
        st_out = [sem(f"st_out{i}") for i in range(2)]
        c_ident, c_zero, c_const, c_ones = sem("c_ident"), sem("c_zero"), sem("c_const"), sem("c_ones")
        c_pick, c_half = sem("c_pick"), sem("c_half")
        c_pool, c_rope = sem("c_pool"), sem("c_rope")
        m_exp, m_dve, m_silu, m_cols, m_cols_s = sem("m_exp"), sem("m_dve"), sem("m_silu"), sem("m_cols"), sem("m_cols_s")
        m_mod, m_rows, m_rows_s, m_gdve, m_gates = sem("m_mod"), sem("m_rows"), sem("m_rows_s"), sem("m_gdve"), sem("m_gates")
        p_xT, p_qk, p_v, p_kq = sem("p_xT"), sem("p_qk"), sem("p_v"), sem("p_kq")
        p_s, p_sT, p_pv = sem("p_s"), sem("p_sT"), sem("p_pv")
        p_o, p_onT, p_wo, p_h2T, p_lg = sem("p_o"), sem("p_onT"), sem("p_wo"), sem("p_h2T"), sem("p_lg")
        p_mask, p_up, p_down = sem("p_mask"), sem("p_up"), sem("p_down")
        a_hi = sem("a_hi")
        a_hT, a_qk, a_ssq, a_v, a_k, a_q = sem("a_hT"), sem("a_qk"), sem("a_ssq"), sem("a_v"), sem("a_k"), sem("a_q")
        a_exp, a_oT, a_onT, a_h2T, a_lsum, a_mask = (sem("a_exp"), sem("a_oT"), sem("a_onT"), sem("a_h2T"),
                                                     sem("a_lsum"), sem("a_mask"))
        v_st1, v_ve1, v_xn, v_ssqe, v_rot, v_rr, v_lo, v_k = (sem("v_st1"), sem("v_ve1"), sem("v_xn"), sem("v_ssqe"),
                                                              sem("v_rot"), sem("v_rr"), sem("v_lo"), sem("v_k"))
        v_pick, v_max, v_sub = sem("v_pick"), sem("v_max"), sem("v_sub")
        v_rden, v_on, v_yg, v_st2, v_ve2, v_xn2 = (sem("v_rden"), sem("v_on"), sem("v_yg"), sem("v_st2"),
                                                   sem("v_ve2"), sem("v_xn2"))
        v_lg, v_gate, v_onehot, v_psel, v_hm, v_z = (sem("v_lg"), sem("v_gate"), sem("v_onehot"), sem("v_psel"),
                                                     sem("v_hm"), sem("v_z"))
        g_rs1, g_rot, g_rqk, g_sel, g_x1, g_rs2, g_out = (sem("g_rs1"), sem("g_rot"), sem("g_rqk"), sem("g_sel"),
                                                          sem("g_x1"), sem("g_rs2"), sem("g_out"))

        W_DMAS = 5

        def scores_of(u):
            b = S_BANK[u]
            return ps[:, b:b + 2, :].rearrange("p b (h t k) -> p (b h) t k", h=2, t=2)

        def bank(b, n):
            return ps[:, b, 0:n]

        def slots(x, i, part):
            return x[:, :, part:4:2, :] if i == 0 else x[:, :, 2 * part:2 * part + 2, :]

        def heads_twice(x):
            return x.rearrange("p (h d) -> p h d", h=NH).unsqueeze(2).to_broadcast([P, NH, 2, HD])

        block = ctx.enter_context(nc.Block())

        @block.sync
        def _(sp):
            def load_x(t):
                wait(sp, g_x1, t.count(1, -JT + 1))
                sp.dma_start(xs[:, t.j, :], x_t[t.index]).then_inc(ld_x[t.j], 16)

            sp.dma_start(c_s[:, :, :], c_t.rearrange("(k p) b -> p k b", p=P)).then_inc(ld_c, 16)
            load_x(At(0, 0))
            sp.dma_start(wqkv_s[:, :, :], wqkv.rearrange("(k p) n -> p k n", p=P)).then_inc(ld_w, 16)
            load_x(At(0, 1))
            sp.dma_start(wo_s[:, :, :], wo.rearrange("(k p) n -> p k n", p=P)).then_inc(ld_w, 16)
            sp.dma_start(gate_s[:, :, :], gate_t.rearrange("(k p) n -> p k n", p=P)).then_inc(ld_w, 16)
            sp.dma_start(up_s[:, :, :], up_t.rearrange("(k p) n -> p k n", p=P)).then_inc(ld_w, 16)
            sp.dma_start(down_s[:, :, :], down.rearrange("(k p) n -> p k n", p=P)).then_inc(ld_w, 16)

            def slot(seq, r, live):
                ahead, g = At(seq, r + 2), At(seq, r - 3)
                if not ahead.peeled or ahead.index < TILES:
                    load_x(ahead)
                if "G" in live:
                    wait(sp, g_out, g.count(1, 1))
                    sp.dma_start(out_t[g.index], obuf[:, g.k % 2, :]).then_inc(st_out[g.k % 2], 16)

            run_slots(sp, slot)
            for i in range(2):
                sp.wait_ge(st_out[i], 16 * TILES // 2)

        @block.tensor
        def _(pe):
            def transposes(dst, srcs, done):
                for i, src in enumerate(srcs):
                    last = pe.transpose(dst[:, i * P:(i + 1) * P], src, ident[:, :])
                last.then_inc(done, 1)

            def project(dst, lhs_t, rhs, parts, done):
                for k in range(parts):
                    last = pe.matmul(dst, lhs_t(k), rhs(k), start=(k == 0), stop=(k == parts - 1))
                last.then_inc(done, 1)

            pe.wait_ge(ld_mod, 16)
            pe.wait_ge(m_silu, 1)
            for i, m in enumerate((0, 1, 3, 4)):
                for h in range(DC):
                    for k in range(DC):
                        o = (i * DC + h) * BATCH
                        last = pe.matmul(ps[:, 0, o:o + BATCH], wmod_s[:, k, m * D + h * P:m * D + (h + 1) * P],
                                         silu[:, k, :], start=(k == 0), stop=(k == DC - 1))
            last.then_inc(m_cols, 1)
            pe.wait_ge(c_ident, 2)

            def gate_rows():
                pe.wait_ge(m_silu, 2)
                pe.wait_ge(m_cols_s, 1)
                for b in range(BATCH):
                    for k in range(DC):
                        last = pe.matmul(ps[:, b, :], silu_rows[:, k, b, :],
                                         wmod_s[:, k, :].rearrange("p (a m n) -> p a m n", a=2, m=3)[:, :, 2, :],
                                         start=(k == 0), stop=(k == DC - 1))
                    last.then_inc(m_rows, 1)

            def scores(t, c):
                u = c % 2
                wait(pe, v_sub, t.count(NC, c - 1))
                if t.peeled and t.index == 0 and c < 2:
                    pe.wait_ge(m_rows_s, BATCH)
                wait(pe, a_q, t.count(2, 2))
                wait(pe, a_k, t.count(2, 2))
                wait(pe, v_k, t.count(2, 2))
                if t.peeled and t.index == 0:
                    pe.wait_ge(c_half, 1)
                for i in range(2):
                    g = 2 * c + i
                    dst = ps[:, S_BANK[u] + i, :].rearrange("p (h n) -> p h n", h=2)
                    if t.j == 0:
                        dst, keys = dst[:, :, P:2 * P], kT[:, g, :, 0, :]
                    else:
                        keys = kT[:, g, :, t.j - 1:t.j + 1, :].rearrange("p h t k -> p h (t k)")
                    last = pe.matmul(dst, qT[:, g, :], keys, start=True, stop=True)
                last.then_inc(p_s, 1)

            def scores_T(t, c):
                wait(pe, a_oT, t.count(NC, c - 1))
                wait(pe, v_sub, t.count(NC, c + 1))
                transposes(ps[:, PT_BANK[c % 2], :], [shifted[:, c % 2, i, :] for i in range(CH)], p_sT)

            def values(t, c):
                wait(pe, a_v, t.count(1, 1))
                wait(pe, g_sel, t.count(NC, c + 1))
                if t.j > 0:
                    for i in range(CH):
                        pe.matmul(ps[32 * i:32 * i + VW, PT_BANK[c % 2], 0:P], v_s[:, t.j - 1, CH * c + i, :],
                                  prev_p[:, c % 2, i, :], start=True, stop=False)
                for i in range(CH):
                    last = pe.matmul(ps[32 * i:32 * i + VW, PT_BANK[c % 2], 0:P], v_s[:, t.j, CH * c + i, :],
                                     own_p[:, c % 2, i, :], start=(t.j == 0), stop=True)
                last.then_inc(p_pv, 1)

            def qk_T(p, n):
                wait(pe, a_hi, p.count(2, 2))
                wait(pe, v_lo, p.count(2, 2))
                srcs = []
                for g in range(CH * (n % 2), CH * (n % 2) + CH):
                    pair = hilo[:, 1 if n < 2 else 0, 2 * g:2 * g + 2, :, :].bitcast(F32)
                    srcs.append(pair.rearrange("p h s d -> p (h s d)"))
                transposes(ps[:, W7, :], srcs, p_kq)

            def slot(seq, r, live):
                p, t, f, g = (At(seq, r - lag) for lag in range(4))
                if "T" in live:
                    scores(t, 0)
                if "P" in live:
                    wait(pe, v_lg, f.count(1, 0))
                    wait(pe, a_v, p.count(1, 0))
                    wait(pe, v_xn, p.count(1, 1))
                    transposes(ps[:, W6, :], [xn[:, k * P:(k + 1) * P] for k in range(DC)], p_xT)
                if "T" in live:
                    scores(t, 1)
                if "G" in live:
                    if p.peeled and p.index > TILES:
                        wait(pe, v_hm, g.count(1, 0))
                    else:
                        wait(pe, a_q, p.count(2, 0))
                    wait(pe, v_onehot, g.count(1, 1))
                    for i in range(EC):
                        chosen = onehot[:, :, :].rearrange("p e r -> p (e r)")[:, i * P:(i + 1) * P]
                        last = pe.matmul(ps[:, W7, i * P:(i + 1) * P], chosen, ident_b[:, :], start=True, stop=True)
                    last.then_inc(p_mask, 1)
                if "P" in live:
                    if p.peeled and p.index == 0:
                        pe.wait_ge(ld_w, 16 * W_DMAS)
                    wait(pe, a_hT, p.count(1, 1))
                    project(ps[:, W6, :], lambda k: hT[:, k, :], lambda k: wqkv_s[:, k, 0:2 * D], DC, p_qk)
                if "T" in live:
                    scores_T(t, 0)
                if "F" in live:
                    wait(pe, *((a_mask, g.count(1, 1)) if "G" in live else (a_q, p.count(2, 0))))
                    wait(pe, a_oT, f.count(NC, NC))
                    transposes(ps[:, W7, :], [oT[:, i, :] for i in range(NC)], p_o)
                if "T" in live:
                    scores(t, 2)
                if "P" in live:
                    wait(pe, a_qk, p.count(1, 1))
                    project(ps[:, W6, 0:D], lambda k: hT[:, k, :], lambda k: wqkv_s[:, k, 2 * D:3 * D], DC, p_v)
                if "T" in live:
                    scores_T(t, 1)
                if "G" in live:
                    wait(pe, *((v_on, f.count(1, 1)) if "F" in live else (a_mask, g.count(1, 1))))
                    for i in range(EC):
                        for k in range(DC):
                            last = pe.matmul(ps[:, W7, i * P:(i + 1) * P], up_s[:, k, i * P:(i + 1) * P],
                                             h2T[:, k, :], start=(k == 0), stop=(k == DC - 1))
                    last.then_inc(p_up, 1)
                if "F" in live:
                    wait(pe, *((a_v, p.count(1, 1)) if "P" in live else (v_lg, f.count(1, 0))))
                    wait(pe, v_on, f.count(1, 1))
                    flat = on[:, :, :].rearrange("p h d -> p (h d)")
                    transposes(ps[:, W6, :], [flat[:, k * P:(k + 1) * P] for k in range(DC)], p_onT)
                if "T" in live:
                    values(t, 0)
                    scores(t, 3)
                    scores_T(t, 2)
                if "P" in live:
                    wait(pe, *((v_hm, g.count(1, 1)) if "G" in live else
                               (v_on, f.count(1, 1)) if "F" in live else (a_q, p.count(2, 0))))
                    qk_T(p, 0)
                if "F" in live:
                    wait(pe, a_onT, f.count(1, 1))
                    project(ps[:, W6, 0:D], lambda k: onT[:, k, :], lambda k: wo_s[:, k, :], DC, p_wo)
                if "T" in live:
                    values(t, 1)
                    scores_T(t, 3)
                if "P" in live:
                    wait(pe, a_k, p.count(2, 1))
                    wait(pe, v_k, p.count(2, 1))
                    qk_T(p, 1)
                if "G" in live:
                    wait(pe, *((v_yg, f.count(1, 1)) if "F" in live else (v_lg, f.count(1, 0))))
                    wait(pe, v_hm, g.count(1, 1))
                    project(ps[:, W6, 0:D], lambda k: hm[:, k, :], lambda k: down_s[:, k, :], EC, p_down)
                if "T" in live:
                    values(t, 2)
                if "P" in live:
                    wait(pe, a_k, p.count(2, 2))
                    wait(pe, v_k, p.count(2, 2))
                    wait(pe, a_q, p.count(2, 0))
                    qk_T(p, 2)
                if "F" in live:
                    wait(pe, *((v_z, g.count(1, 1)) if "G" in live else (v_yg, f.count(1, 1))))
                    wait(pe, v_xn2, f.count(1, 1))
                    transposes(ps[:, W6, :], [xn2[:, k * P:(k + 1) * P] for k in range(DC)], p_h2T)
                if "P" in live:
                    wait(pe, a_q, p.count(2, 1))
                    qk_T(p, 3)
                if "F" in live:
                    wait(pe, a_h2T, f.count(1, 1))
                    project(ps[:, W6, 0:EXPERTS], lambda k: h2T[:, k, :], lambda k: gate_s[:, k, :], DC, p_lg)
                if "T" in live:
                    values(t, 3)
                if p.peeled and p.index == 0:
                    gate_rows()

            run_slots(pe, slot)

        @block.scalar
        def _(act):
            target = act.alloc_register("act_target")
            act.dma_start(wmod_s[:, :, :], wmod.rearrange("(k p) n -> p k n", p=P)).then_inc(ld_mod, 16)
            act.dma_start(trig_s[:, :, :, :, :], trig.rearrange("(j p) a b d -> p j a b d", p=P)).then_inc(ld_trig, 16)
            act.dma_start(normw[:, 0, :], qw.partition_broadcast(P)).then_inc(ld_trig, 16)
            act.dma_start(normw[:, 1, :], kw.partition_broadcast(P)).then_inc(ld_trig, 16)
            act.wait_ge(ld_c, 16)
            act.activation(ec[:, :, :], c_s[:, :, :], ACT.Exp, scale=-1.0).then_inc(m_exp, 1)
            act.wait_ge(m_cols, 1)
            act.activation(mod_s[:, :, :, :].rearrange("p m h b -> p (m h b)"), ps[:, 0, 0:4 * DC * BATCH],
                           ACT.Identity).then_inc(m_cols_s, 1)
            act.wait_ge(m_mod, 1)

            def modulate(dst, which, at, done):
                b = at.sequence
                for h in range(DC):
                    last = act.activation(dst[:, h, :], ps[:, W6, h * P:(h + 1) * P], ACT.Identity,
                                          scale=mod_s[:, 2 * which + 1, h, bass.ds(b, 1)],
                                          bias=mod_s[:, 2 * which, h, bass.ds(b, 1)])
                last.then_inc(done, 1)

            def slot(seq, r, live):
                p, t, f, g = (At(seq, r - lag) for lag in range(4))

                def exps(c):
                    wait(act, g_sel, t.count(NC, c - 1))
                    wait(act, p_sT, t.count(NC, c + 1))
                    act.activation(expT[:, c % 2, :, :].rearrange("p h q -> p (h q)"), ps[:, PT_BANK[c % 2], :],
                                   ACT.Exp).then_inc(a_exp, 1)

                def out_T(c):
                    wait(act, p_o, t.count(1, 0))
                    wait(act, p_pv, t.count(NC, c + 1))
                    act.activation(oT[:, c, :], ps[:, PT_BANK[c % 2], 0:P], ACT.Identity).then_inc(a_oT, 1)

                def k_even(n):
                    wait(act, p_s, p.count(NC, -2 * NC))
                    wait(act, p_kq, p.count(4, n + 1))
                    act.activation(kT[0:64, CH * n:CH * n + CH, 0, p.j, :],
                                   ps[0:64, W7, :].rearrange("p (g k) -> p g k", g=CH), ACT.Identity).then_inc(a_k, 1)

                def q_rows(n):
                    wait(act, p_s, p.count(NC, 0))
                    wait(act, p_kq, p.count(4, 3 + n))
                    act.activation(qT[:, CH * n:CH * n + CH, :].rearrange("p g k -> p (g k)"), ps[:, W7, :],
                                   ACT.Identity).then_inc(a_q, 1)

                if "P" in live:
                    wait(act, p_v, p.count(1, 0))
                    wait_alone(act, p_xT, p.count(1, 1), target, m_mod)
                    modulate(hT, 0, p, a_hT)
                if "G" in live:
                    wait(act, v_hm, g.count(1, 0))
                    wait(act, p_mask, g.count(1, 1))
                    act.activation(maskT[:, :, :].rearrange("p e t -> p (e t)"), ps[:, W7, :],
                                   ACT.Identity).then_inc(a_mask, 1)
                if "P" in live:
                    wait(act, g_rot, p.count(3, 0))
                    wait(act, p_qk, p.count(1, 1))
                    act.activation(qk[:, :, :].rearrange("p a d -> p (a d)"), ps[:, W6, :],
                                   ACT.Identity).then_inc(a_qk, 1)
                    wait(act, a_qk, p.count(1, 1))
                    wait(act, v_ssqe, p.count(1, 0))
                    for i in range(2):
                        wait(act, a_ssq, p.count(2, i))
                        act.activation(sq[:, :], qk[:, i, :], ACT.Square, accum_out=ssq[:, i:i + 1]).then_inc(a_ssq, 1)
                if "T" in live:
                    exps(0)
                if "P" in live:
                    wait(act, p_pv, p.count(NC, -2 * NC))
                    if p.peeled and p.index == 0:
                        act.wait_ge(c_ones, 1)
                    wait(act, p_v, p.count(1, 1))
                    act.activation(v_s[:, p.j, :, 0:HD], ps[:, W6, 0:D].rearrange("p (h d) -> p h d", h=NH),
                                   ACT.Identity).then_inc(a_v, 1)
                if "T" in live:
                    exps(1)
                if "F" in live:
                    wait(act, p_wo, f.count(1, 0))
                    wait(act, p_onT, f.count(1, 1))
                    act.activation(onT[:, :, :].rearrange("p k t -> p (k t)"), ps[:, W6, 0:D],
                                   ACT.Identity).then_inc(a_onT, 1)
                if "P" in live:
                    wait(act, p_kq, p.count(4, 0))
                    wait(act, g_rqk, p.count(1, 1))
                    wait(act, v_rot, p.count(1, 1))
                    for i in range(2):
                        act.activation(slots(hilo[:, i, :, :, :], i, 0), heads_twice(rot[:, i, :]), ACT.Identity,
                                       scale=rqk[:, i:i + 1]).then_inc(a_hi, 1)
                if "T" in live:
                    out_T(0)
                    exps(2)
                if "P" in live:
                    k_even(0)
                if "T" in live:
                    out_T(1)
                    exps(3)
                if "P" in live:
                    k_even(1)
                if "T" in live:
                    out_T(2)
                if "P" in live:
                    q_rows(0)
                if "F" in live:
                    wait(act, p_up, f.count(1, 0))
                    wait_alone(act, p_h2T, f.count(1, 1), target, m_mod)
                    modulate(h2T, 1, f, a_h2T)
                if "P" in live:
                    q_rows(1)
                if "T" in live:
                    out_T(3)
                if "F" in live:
                    wait(act, v_psel, f.count(1, 0))
                    wait(act, v_gate, f.count(4, 1))
                    act.activation(lexp[:, :], lgs[:, :], ACT.Exp, bias=nmx[:, :], accum_out=lsum[:, :]).then_inc(a_lsum, 1)
                if p.peeled and p.index == 0:
                    for b in range(BATCH):
                        act.wait_ge(m_rows, b + 1)
                        act.activation(gates[:, b, :, :].rearrange("p a n -> p (a n)"), ps[:, b, :],
                                       ACT.Identity).then_inc(m_rows_s, 1)

            run_slots(act, slot)

        @block.vector
        def _(dve):
            target = dve.alloc_register("dve_target")
            dve.memset(kT[0:64, :, 1, :, :].bitcast(F32), 0.0).then_inc(c_zero, 1)
            dve.wait_ge(m_exp, 1)
            dve.tensor_scalar(ec1[:, :, :], ec[:, :, :], 1.0, None, ALU.add).then_inc(m_dve, 1)
            dve.wait_ge(m_dve, 1)
            dve.reciprocal(sig[:, :, :], ec1[:, :, :]).then_inc(m_dve, 1)
            dve.wait_ge(m_dve, 2)
            dve.tensor_tensor(silu[:, :, :], c_s[:, :, :], sig[:, :, :], ALU.mult).then_inc(m_silu, 1)
            dve.wait_ge(m_silu, 1)
            dve.tensor_copy(silu_rows[:, :, :, :], silu[:, :, :].unsqueeze(3).to_broadcast([P, DC, BATCH, P])).then_inc(m_silu, 1)

            def stats(src, st, mv, ve, s_st, s_ve, at):
                dve.bn_stats(out=st[:, :], in_=src).then_inc(s_st, 1)
                wait_alone(dve, s_st, at.count(2, 1), target, c_zero)
                dve.bn_aggr(out=mv[:, :], in_=st[:, :]).then_inc(s_st, 1)
                wait(dve, s_st, at.count(2, 2))
                dve.tensor_scalar(ve[:, :], mv[:, 1:2], EPS_LN, None, ALU.add).then_inc(s_ve, 1)

            def normed(dst, src, mv, rs, done):
                dve.tensor_scalar(dst[:, :], src, mv[:, 0:1], rs[:, 0:1], ALU.subtract, ALU.mult).then_inc(done, 1)

            def ln1_stats(at):
                if at.peeled:
                    dve.wait_ge(ld_x[at.j], 16 * (at.sequence + 1))
                else:
                    dve.wait_ge(ld_x[at.j], at.sequence * 16 + 16)
                wait(dve, g_rs1, at.count(1, 0))
                stats(xs[:, at.j, :], st1, mv1, ve1, v_st1, v_ve1, at)

            def ln1(at):
                wait(dve, p_xT, at.count(1, 0))
                wait(dve, g_rs1, at.count(1, 1))
                normed(xn, xs[:, at.j, :], mv1, rs1, v_xn)

            ln1_stats(At(0, 0))
            dve.wait_ge(c_pool, 1)
            dve.tensor_copy(take_prev[:, :], take_f[:, :]).then_inc(c_pick, 1)
            dve.wait_ge(m_cols_s, 1)
            dve.tensor_scalar(mod_s[:, 1:4:2, :, :], mod_s[:, 1:4:2, :, :], 1.0, None, ALU.add).then_inc(m_mod, 1)
            ln1(At(0, 0))
            dve.wait_ge(ld_trig, 48)
            for i in range(2):
                w = normw[:, i, :].rearrange("p (h d) -> p h d", h=NH)
                dve.tensor_tensor(cosw[:, :, i, :].rearrange("p j (h d) -> p j h d", h=NH),
                                  w.unsqueeze(1).to_broadcast([P, JT, NH, HD]),
                                  trig_s[:, :, i, 0, :].unsqueeze(2).to_broadcast([P, JT, NH, HD]),
                                  ALU.mult).then_inc(c_rope, 1)
                for a in range(2):
                    dve.tensor_tensor(
                        sinw[:, :, i, :].rearrange("p j (h a d) -> p j h a d", h=NH, a=2)[:, :, :, a, :],
                        w[:, :, HALF * (1 - a):HALF * (2 - a)].unsqueeze(1).to_broadcast([P, JT, NH, HALF]),
                        trig_s[:, :, i, 1, HALF * a:HALF * (a + 1)].unsqueeze(2).to_broadcast([P, JT, NH, HALF]),
                        ALU.mult).then_inc(c_rope, 1)

            def gate_values():
                n = 0
                for b in range(BATCH):
                    raw = gates[:, b, :, :].rearrange("p a n -> p (a n)")
                    dve.wait_ge(m_rows_s, b + 1)
                    if b:
                        dve.wait_ge(m_gates, b)
                    dve.tensor_scalar(gsgn[:, :], raw, 0.0, 2.0, ALU.is_ge, ALU.mult).then_inc(m_gdve, 1)
                    dve.scalar_tensor_tensor(out=gtmp[:, :], in0=raw, scalar=-1.0, in1=raw, op0=ALU.mult,
                                             op1=ALU.max).then_inc(m_gdve, 1)
                    n += 2
                    dve.wait_ge(m_gdve, n)
                    dve.tensor_scalar(gtmp[:, 0:D], gtmp[:, 0:D], 0.25, None, ALU.max).then_inc(m_gdve, 1)
                    dve.tensor_scalar(gtmp[:, D:2 * D], gtmp[:, D:2 * D], 0.25, SCALING, ALU.max,
                                      ALU.mult).then_inc(m_gdve, 1)
                    n += 2
                    dve.wait_ge(m_gdve, n)
                    dve.scalar_tensor_tensor(out=raw, in0=gsgn[:, :], scalar=-1.0, in1=gtmp[:, :], op0=ALU.add,
                                             op1=ALU.mult).then_inc(m_gates, 1)

            def slot(seq, r, live):
                l, p, t, f, g = (At(seq, r - lag) for lag in range(-1, 4))

                def softmax(c):
                    u = c % 2
                    s = scores_of(u)
                    own = s[:, :, 1, :]
                    pick = take_prev[:, :].unsqueeze(1).to_broadcast([P, CH, P])
                    other = s[:, :, 0, :] if t.j else neg_s[:, :].unsqueeze(1).to_broadcast([P, CH, P])
                    if t.peeled and t.index == 0:
                        dve.wait_ge(c_pick, 1)
                        dve.wait_ge(c_ones, 1)
                    wait_alone(dve, p_s, t.count(NC, c + 1), target, c_zero)
                    dve.copy_predicated(own, pick, other).then_inc(v_pick, 1)
                    wait(dve, v_pick, t.count(NC, c + 1))
                    dve.tensor_reduce(negm[:, u, :], own, AX.X, ALU.max, negate=True).then_inc(v_max, 1)
                    wait(dve, v_max, t.count(NC, c + 1))
                    wait(dve, p_sT, t.count(NC, c - 1))
                    dve.tensor_tensor(shifted[:, u, :, :], own, negm[:, u, :].unsqueeze(2).to_broadcast([P, CH, P]),
                                      ALU.add).then_inc(v_sub, 1)

                def k_odd(n):
                    wait(dve, p_s, p.count(NC, -2 * NC))
                    wait(dve, p_kq, p.count(4, n + 1))
                    dve.tensor_copy(kT[64:128, CH * n:CH * n + CH, 1, p.j, :],
                                    ps[64:128, W7, :].rearrange("p (g k) -> p g k", g=CH)).then_inc(v_k, 1)

                if "T" in live:
                    softmax(0)
                    softmax(1)
                if "P" in live:
                    wait(dve, a_ssq, p.count(2, 2))
                    wait(dve, g_rqk, p.count(1, 0))
                    dve.tensor_scalar(ssqe[:, :], ssq[:, :], 1.0 / D, EPS_RMS, ALU.mult, ALU.add).then_inc(v_ssqe, 1)
                if "F" in live:
                    heads = ps[:, W7, :].rearrange("p (h d) -> p h d", h=NH)
                    wait(dve, p_o, f.count(1, 1))
                    dve.reciprocal(rden[:, :], heads[:, :, HD]).then_inc(v_rden, 1)
                    wait(dve, v_rden, f.count(1, 1))
                    wait(dve, p_onT, f.count(1, 0))
                    dve.tensor_tensor(on[:, :, :], heads[:, :, 0:HD],
                                      rden[:, :].unsqueeze(2).to_broadcast([P, NH, HD]), ALU.mult).then_inc(v_on, 1)
                if "T" in live:
                    softmax(2)
                if "G" in live:
                    wait(dve, a_mask, g.count(1, 1))
                    wait(dve, p_down, g.count(1, 0))
                    wait(dve, p_up, g.count(1, 1))
                    dve.tensor_tensor(hm[:, :, :].rearrange("p e t -> p (e t)"), ps[:, W7, :],
                                      maskT[:, :, :].rearrange("p e t -> p (e t)"), ALU.mult).then_inc(v_hm, 1)
                if "L" in live:
                    ln1_stats(l)
                if "P" in live:
                    flat = [x.rearrange("p a d -> p (a d)") for x in (rot[:, :, :], t1[:, :, :], t2[:, :, :])]
                    wait(dve, a_hi, p.count(2, 0))
                    wait(dve, g_rot, p.count(3, 3))
                    dve.tensor_tensor(*flat, ALU.add).then_inc(v_rot, 1)
                    wait(dve, v_rot, p.count(1, 1))
                    wait(dve, g_rqk, p.count(1, 1))
                    for i in range(2):
                        dve.tensor_scalar(rr[:, i, :], rot[:, i, :], rqk[:, i:i + 1], None, ALU.mult).then_inc(v_rr, 1)
                    wait(dve, v_rr, p.count(2, 2))
                    wait(dve, p_kq, p.count(4, 0))
                    for i in range(2):
                        wait(dve, a_hi, p.count(2, 1 + i))
                        dve.tensor_tensor(slots(hilo[:, i, :, :, :], i, 1), heads_twice(rr[:, i, :]),
                                          slots(hilo[:, i, :, :, :], i, 0).bitcast(F32), ALU.subtract).then_inc(v_lo, 1)
                if "T" in live:
                    softmax(3)
                if "P" in live:
                    k_odd(0)
                if "F" in live:
                    if f.peeled and f.index == 0:
                        dve.wait_ge(m_gates, BATCH)
                    wait(dve, g_x1, f.count(1, 0))
                    wait(dve, p_wo, f.count(1, 1))
                    dve.tensor_tensor(yg[:, :], ps[:, W6, 0:D], gates[:, f.sequence, 0, :], ALU.mult).then_inc(v_yg, 1)
                if "P" in live:
                    k_odd(1)
                if "F" in live:
                    wait(dve, g_rs2, f.count(1, 0))
                    wait(dve, g_x1, f.count(1, 1))
                    stats(x1[:, f.k % 2, :], st2, mv2, ve2, v_st2, v_ve2, f)
                if "G" in live:
                    wait(dve, g_out, g.count(1, 0))
                    wait(dve, v_psel, g.count(1, 1))
                    wait(dve, p_down, g.count(1, 1))
                    dve.scalar_tensor_tensor(out=z[:, :], in0=ps[:, W6, 0:D], scalar=psel[:, :],
                                             in1=gates[:, g.sequence, 1, :], op0=ALU.mult, op1=ALU.mult).then_inc(v_z, 1)
                if "F" in live:
                    wait(dve, p_h2T, f.count(1, 0))
                    wait(dve, g_rs2, f.count(1, 1))
                    normed(xn2, x1[:, f.k % 2, :], mv2, rs2, v_xn2)
                if "L" in live:
                    ln1(l)
                if "F" in live:
                    wait(dve, a_lsum, f.count(1, 0))
                    wait(dve, p_lg, f.count(1, 1))
                    dve.tensor_copy(lgs[:, :], ps[:, W6, 0:EXPERTS]).then_inc(v_lg, 1)
                    wait(dve, v_lg, f.count(1, 1))
                    dve.tensor_reduce(nmx[:, :], lgs[:, :], AX.X, ALU.max, negate=True).then_inc(v_gate, 1)
                    wait(dve, v_gate, f.count(4, 1))
                    dve.tensor_scalar(ge[:, :], lgs[:, :], nmx[:, :], 0.0, ALU.add, ALU.is_ge).then_inc(v_gate, 1)
                    wait(dve, v_gate, f.count(4, 2))
                    dve.tensor_tensor(score[:, :], ge[:, :], first_s[:, :], ALU.mult).then_inc(v_gate, 1)
                    wait(dve, v_gate, f.count(4, 3))
                    dve.tensor_reduce(best[:, :], score[:, :], AX.X, ALU.max).then_inc(v_gate, 1)
                    wait(dve, v_gate, f.count(4, 4))
                    wait(dve, p_mask, f.count(1, 0))
                    dve.tensor_scalar(onehot[:, :, :], score[:, :].unsqueeze(2).to_broadcast([P, EXPERTS, RANK]),
                                      best[:, :], None, ALU.is_equal).then_inc(v_onehot, 1)
                    wait(dve, a_lsum, f.count(1, 1))
                    dve.reciprocal(psel[:, :], lsum[:, :]).then_inc(v_psel, 1)
                if p.peeled and p.index == 0:
                    gate_values()

            run_slots(dve, slot)

        @block.gpsimd
        def _(pool):
            target = pool.alloc_register("pool_target")
            pool.memset(ones_f[:, :], 1.0).then_inc(c_const, 1)
            pool.memset(pow_s[:, :], -0.5).then_inc(c_const, 1)
            pool.wait_ge(c_const, 2)
            pool.affine_select(out=ident[:, :], in_=ones_f[:, :], compare_op=ALU.is_equal, fill=0.0, base=0,
                               pattern=[[1, P]], channel_multiplier=-1).then_inc(c_ident, 1)
            pool.affine_select(out=ident_b[:, :], in_=ones_f[:, :], compare_op=ALU.is_equal, fill=0.0, base=0,
                               pattern=[[1, P]], channel_multiplier=-1).then_inc(c_ident, 1)
            pool.affine_select(out=take_f[:, :], in_=ones_f[:, :], compare_op=ALU.is_ge, fill=0.0, base=-1,
                               pattern=[[1, P]], channel_multiplier=-1).then_inc(c_pool, 1)
            pool.wait_ge(v_ve1, 1)
            pool.tensor_tensor(rs1[:, :], ve1[:, :], pow_s[:, 0:1], ALU.pow).then_inc(g_rs1, 1)
            pool.memset(neg_s[:, :], NEG)
            for e in range(EXPERTS):
                pool.memset(first_s[:, e:e + 1], float(EXPERTS - e))
            pool.memset(v_s[:, :, :, HD:VW], 1.0).then_inc(c_ones, 1)
            pool.wait_ge(c_ones, 1)
            pool.memset(kT[64:128, :, 0, :, :].bitcast(F32), 0.0).then_inc(c_half, 1)
            pool.wait_ge(c_half, 1)

            def slot(seq, r, live):
                l, p, t, f, g = (At(seq, r - lag) for lag in range(-1, 4))

                def select(c):
                    u = c % 2
                    wait_alone(pool, a_exp, t.count(NC, c + 1), target, c_const)
                    if t.j:
                        pool.affine_select(out=prev_p[:, u, :, :], in_=expT[:, u, :, :], compare_op=ALU.is_ge,
                                           fill=0.0, base=-1, pattern=[[0, CH], [-1, P]], channel_multiplier=1)
                    pool.affine_select(out=own_p[:, u, :, :], in_=expT[:, u, :, :], compare_op=ALU.is_ge,
                                       fill=0.0, base=0, pattern=[[0, CH], [1, P]],
                                       channel_multiplier=-1).then_inc(g_sel, 1)

                if "P" in live:
                    wait(pool, v_rot, p.count(1, 0))
                    if p.peeled and p.index == 0:
                        pool.wait_ge(c_rope, 6)
                    wait(pool, a_qk, p.count(1, 1))
                    pool.tensor_tensor(t1[:, :, :], qk[:, :, :], cosw[:, p.j, :, :], ALU.mult).then_inc(g_rot, 1)
                    halves = [x.rearrange("p i (h a d) -> p (i h) a d", h=NH, a=2)
                              for x in (t2[:, :, :], qk[:, :, :], sinw[:, p.j, :, :])]
                    for a in range(2):
                        pool.tensor_tensor(halves[0][:, :, a, :], halves[1][:, :, 1 - a, :], halves[2][:, :, a, :],
                                           ALU.mult).then_inc(g_rot, 1)
                if "T" in live:
                    select(0)
                if "P" in live:
                    wait(pool, v_rr, p.count(2, 0))
                    wait(pool, a_hi, p.count(2, 0))
                    wait(pool, v_ssqe, p.count(1, 1))
                    pool.tensor_tensor(rqk[:, :], ssqe[:, :], pow_s[:, :], ALU.pow).then_inc(g_rqk, 1)
                if "T" in live:
                    select(1)
                if "L" in live:
                    wait(pool, v_xn, l.count(1, 0))
                    wait(pool, v_ve1, l.count(1, 1))
                    pool.tensor_tensor(rs1[:, :], ve1[:, :], pow_s[:, 0:1], ALU.pow).then_inc(g_rs1, 1)
                if "T" in live:
                    select(2)
                if "F" in live:
                    wait(pool, g_out, f.count(1, -1))
                    wait(pool, v_yg, f.count(1, 1))
                    pool.tensor_tensor(x1[:, f.k % 2, :], xs[:, f.j, :], yg[:, :], ALU.add).then_inc(g_x1, 1)
                if "T" in live:
                    select(3)
                if "F" in live:
                    wait(pool, v_xn2, f.count(1, 0))
                    wait(pool, v_ve2, f.count(1, 1))
                    pool.tensor_tensor(rs2[:, :], ve2[:, :], pow_s[:, 0:1], ALU.pow).then_inc(g_rs2, 1)
                if "G" in live:
                    stored = 16 * ((g.k) // 2)
                    if g.peeled:
                        n = 16 * (g.index // 2)
                        wait(pool, st_out[g.k % 2], n if n else None)
                    else:
                        pool.wait_ge(st_out[g.k % 2], seq * (16 * JT // 2) + stored)
                    wait(pool, v_z, g.count(1, 1))
                    pool.tensor_tensor(obuf[:, g.k % 2, :], x1[:, g.k % 2, :], z[:, :], ALU.add).then_inc(g_out, 1)

            run_slots(pool, slot)


def rotation_tables():
    inv = (1.0 / np.float32(10000.0) ** (np.arange(0, HD, 2, dtype=np.float32) / np.float32(HD))).astype(np.float32)
    angle = np.arange(SEQ, dtype=np.float32)[:, None] * inv[None, :]
    cos, sin = np.cos(angle).astype(np.float32), np.sin(angle).astype(np.float32)
    k = np.stack([np.concatenate([cos, cos], 1), np.concatenate([-sin, sin], 1)], 1)
    return np.ascontiguousarray(np.stack([k * np.float32(HD ** -0.5), k], 1))


def kernel(L0_attn_hidden_states, L0_attn_Wqkv, L0_attn_q_norm_w, L0_attn_k_norm_w, L0_attn_Wo, L0_ffn_A,
           L0_ffn_Bw, L0_ffn_Wg, L0_c, L0_wmod):
    import concourse.bacc as bacc
    from concourse.bass_utils import run_bass_kernel_spmd

    arrays = {
        "x": np.asarray(L0_attn_hidden_states).reshape(BATCH * SEQ, D),
        "c_t": np.asarray(L0_c).T,
        "wmod": np.asarray(L0_wmod),
        "wqkv": np.asarray(L0_attn_Wqkv),
        "qw": np.asarray(L0_attn_q_norm_w),
        "kw": np.asarray(L0_attn_k_norm_w),
        "wo": np.asarray(L0_attn_Wo),
        "up_t": np.asarray(L0_ffn_A).reshape(ER, D).T,
        "down": np.asarray(L0_ffn_Bw).transpose(0, 2, 1).reshape(ER, D),
        "gate_t": np.asarray(L0_ffn_Wg).T,
        "trig": rotation_tables(),
    }
    arrays = {n: np.ascontiguousarray(a) for n, a in arrays.items()}
    nc = bacc.Bacc("TRN2", target_bir_lowering=False, num_devices=1)
    ins = [nc.dram_tensor(n, a.shape, mybir.dt.from_np(a.dtype), kind="ExternalInput").ap() for n, a in arrays.items()]
    out = nc.dram_tensor("out", (BATCH * SEQ, D), F32, kind="ExternalOutput").ap()
    build(nc, *ins, out)
    r = run_bass_kernel_spmd(nc, [arrays], core_ids=[0])
    return r.results[0]["out"].reshape(BATCH, SEQ, D)
```

```python
from contextlib import ExitStack

import numpy as np
import concourse.bass as bass
from concourse import mybir

F32 = mybir.dt.float32
F32R = mybir.dt.float32r
BF16 = mybir.dt.bfloat16
U8 = mybir.dt.uint8
ALU = mybir.AluOpType
ACT = mybir.ActivationFunctionType
AX = mybir.AxisListType

P = 128
BATCH, SEQ, D = 4, 512, 256
NH, HD = 16, 16
HALF = HD // 2
JT = SEQ // P
TILES = BATCH * JT
DC = D // P
EXPERTS, RANK = 8, 64
ER = EXPERTS * RANK
EC = ER // P
CH = 4
NC = NH // CH
NG = NH // 2
VW = HD + 1
NEG = -1.0e30
EPS_RMS, EPS_LN = 1e-6, 1e-5
SCALING = 64.0 / 16.0

S_BANK = (0, 2)
PT_BANK = (4, 5)
W6, W7 = 6, 7


class At:

    def __init__(self, seq, k):
        self.seq, self.k = seq, k
        self.peeled = isinstance(seq, int)
        self.j = k % JT
        self.index = seq * JT + k
        self.sequence = seq + k // JT

    def count(self, per=1, extra=0):
        least = (self.seq if self.peeled else 1) * JT * per + self.k * per + extra
        if self.peeled:
            return least if least > 0 else None
        assert least > 0
        return self.seq * (JT * per) + (self.k * per + extra)


def wait(eng, sem, value):
    if value is not None:
        eng.wait_ge(sem, value)


def wait_alone(eng, sem, value, target, done):
    if value is None or isinstance(value, int):
        wait(eng, sem, value)
    else:
        eng.reg_mov(target, value)
        eng.wait_ge(done, 1)
        eng.wait_ge(sem, target)


STAGES = (("L", -2), ("X", -1), ("P", 0), ("T", 1), ("F", 2), ("G", 3))


def run_slots(eng, slot):
    def live(s):
        return {n for n, lag in STAGES if 0 <= s - lag < TILES}
    for r in range(JT):
        slot(0, r, live(r))
    with eng.Fori(1, BATCH - 1) as seq:
        for r in range(JT):
            slot(seq, r, live(JT + r))
    for r in range(JT + 3):
        slot(BATCH - 1, r, live(TILES - JT + r))


def build(nc, x, c_t, wmod, wqkv, qw, kw, wo, up_t, down, gate_t, trig, out):
    x_t = x.rearrange("(n p) d -> n p d", p=P)
    out_t = out.rearrange("(n p) d -> n p d", p=P)
    with ExitStack() as ctx:
        def sb(name, shape, dt=F32):
            return ctx.enter_context(nc.sbuf_tensor(name, shape, dt))

        def sem(name):
            return ctx.enter_context(nc.semaphore(name))

        ps = ctx.enter_context(nc.psum_tensor("ps", [P, 8, 512], F32))

        wqkv_s = sb("wqkv_s", [P, DC, 3 * D])
        wo_s = sb("wo_s", [P, DC, D])
        wmod_s = sb("wmod_s", [P, DC, 6 * D])
        up_s = sb("up_s", [P, DC, ER])
        down_s = sb("down_s", [P, EC, D])
        gate_s = sb("gate_s", [P, DC, EXPERTS])
        c_s = sb("c_s", [P, DC, BATCH])
        trig_s = sb("trig_s", [P, JT, 2, 2, HD])
        normw = sb("normw", [P, 2, D])
        ident = sb("ident", [P, P])
        ident_b = sb("ident_b", [P, P], BF16)
        ones_f = sb("ones_f", [P, P])
        take_prev = sb("take_prev", [P, P], U8)
        take_f = sb("take_f", [P, P])
        neg_s = sb("neg_s", [P, P])
        pow_s = sb("pow_s", [P, 2])
        first_s = sb("first_s", [P, EXPERTS])
        cosw = sb("cosw", [P, JT, 2, D])
        sinw = sb("sinw", [P, JT, 2, D])
        ec = sb("ec", [P, DC, BATCH])
        ec1 = sb("ec1", [P, DC, BATCH])
        sig = sb("sig", [P, DC, BATCH])
        silu = sb("silu", [P, DC, BATCH])
        silu_rows = sb("silu_rows", [P, DC, BATCH, P])
        mod_s = sb("mod_s", [P, 4, DC, BATCH])
        gates = sb("gates", [P, BATCH, 2, D])
        gtmp = sb("gtmp", [P, 2 * D])
        gsgn = sb("gsgn", [P, 2 * D])
        xs = sb("xs", [P, BATCH, JT, D])
        st1 = sb("st1", [P, 6])
        mv1 = sb("mv1", [P, 2])
        ve1 = sb("ve1", [P, 1])
        rs1 = sb("rs1", [P, 1])
        xn = sb("xn", [P, D])
        hT = sb("hT", [P, DC, P])
        qk = sb("qk", [P, 2, D])
        sq = sb("sq", [P, D])
        ssq = sb("ssq", [P, 2])
        ssqe = sb("ssqe", [P, 2])
        rqk = sb("rqk", [P, 2])
        t1 = sb("t1", [P, 2, D])
        t2 = sb("t2", [P, 2, D])
        rot = sb("rot", [P, 2, D])
        rr = sb("rr", [P, 2, D])
        hilo = sb("hilo", [P, 2, NH, 4, HD], F32R)
        qT = sb("qT", [P, NG, P], F32R)
        kT = sb("kT", [P, NG, 2, JT, P], F32R)
        v_s = sb("v_s", [P, JT, NH, VW])
        negm = sb("negm", [P, 2, CH])
        shifted = sb("shifted", [P, 2, CH, P])
        expT = sb("expT", [P, 2, CH, P])
        own_p = sb("own_p", [P, 2, CH, P])
        prev_p = sb("prev_p", [P, 2, CH, P])
        oT = sb("oT", [P, NC, P])
        rden = sb("rden", [P, NH])
        on = sb("on", [P, NH, HD])
        onT = sb("onT", [P, DC, P])
        y = sb("y", [P, D])
        yg = sb("yg", [P, D])
        x1 = sb("x1", [P, 2, D])
        st2 = sb("st2", [P, 6])
        mv2 = sb("mv2", [P, 2])
        ve2 = sb("ve2", [P, 1])
        rs2 = sb("rs2", [P, 1])
        xn2 = sb("xn2", [P, D])
        h2T = sb("h2T", [P, DC, P])
        lgs = sb("lgs", [P, EXPERTS])
        nmx = sb("nmx", [P, 1])
        ge = sb("ge", [P, EXPERTS])
        score = sb("score", [P, EXPERTS])
        best = sb("best", [P, 1])
        onehot = sb("onehot", [P, EXPERTS, RANK], BF16)
        lexp = sb("lexp", [P, EXPERTS])
        lsum = sb("lsum", [P, 1])
        psel = sb("psel", [P, 1])
        maskT = sb("maskT", [P, EC, P], BF16)
        hm = sb("hm", [P, EC, P])
        z = sb("z", [P, D])
        zg = sb("zg", [P, D])
        obuf = sb("obuf", [P, 2, D])

        ld_c, ld_mod, ld_trig, ld_w = sem("ld_c"), sem("ld_mod"), sem("ld_trig"), sem("ld_w")
        ld_x = [sem(f"ld_x{i}") for i in range(3)]
        st_out = [sem(f"st_out{i}") for i in range(2)]
        c_ident, c_zero, c_const, c_ones = sem("c_ident"), sem("c_zero"), sem("c_const"), sem("c_ones")
        c_pick, c_half = sem("c_pick"), sem("c_half")
        c_pool, c_rope = sem("c_pool"), sem("c_rope")
        m_exp, m_dve, m_silu, m_cols, m_cols_s = sem("m_exp"), sem("m_dve"), sem("m_silu"), sem("m_cols"), sem("m_cols_s")
        m_mod, m_rows, m_rows_s, m_gdve, m_gates = sem("m_mod"), sem("m_rows"), sem("m_rows_s"), sem("m_gdve"), sem("m_gates")
        p_xT, p_qk, p_v, p_kq = sem("p_xT"), sem("p_qk"), sem("p_v"), sem("p_kq")
        p_s, p_sT, p_pv = sem("p_s"), sem("p_sT"), sem("p_pv")
        p_o, p_onT, p_wo, p_h2T, p_lg = sem("p_o"), sem("p_onT"), sem("p_wo"), sem("p_h2T"), sem("p_lg")
        p_mask, p_up, p_down = sem("p_mask"), sem("p_up"), sem("p_down")
        a_hi, a_lg, a_y, a_z = sem("a_hi"), sem("a_lg"), sem("a_y"), sem("a_z")
        a_hT, a_qk, a_ssq, a_v, a_k, a_q = sem("a_hT"), sem("a_qk"), sem("a_ssq"), sem("a_v"), sem("a_k"), sem("a_q")
        a_exp, a_oT, a_onT, a_h2T, a_lsum, a_mask = (sem("a_exp"), sem("a_oT"), sem("a_onT"), sem("a_h2T"),
                                                     sem("a_lsum"), sem("a_mask"))
        v_st1, v_ve1, v_xn, v_ssqe, v_rot, v_rr, v_lo, v_k = (sem("v_st1"), sem("v_ve1"), sem("v_xn"), sem("v_ssqe"),
                                                              sem("v_rot"), sem("v_rr"), sem("v_lo"), sem("v_k"))
        v_pick, v_max, v_sub = sem("v_pick"), sem("v_max"), sem("v_sub")
        v_rden, v_on, v_yg, v_st2, v_ve2, v_xn2 = (sem("v_rden"), sem("v_on"), sem("v_yg"), sem("v_st2"),
                                                   sem("v_ve2"), sem("v_xn2"))
        v_lg, v_gate, v_onehot, v_psel, v_hm, v_z = (sem("v_lg"), sem("v_gate"), sem("v_onehot"), sem("v_psel"),
                                                     sem("v_hm"), sem("v_z"))
        g_rs1, g_rot, g_rqk, g_sel, g_x1, g_rs2, g_out, g_yg, g_zg = (sem("g_rs1"), sem("g_rot"), sem("g_rqk"), sem("g_sel"),
                                                          sem("g_x1"), sem("g_rs2"), sem("g_out"), sem("g_yg"), sem("g_zg"))

        W_DMAS = 5

        def scores_of(u):
            b = S_BANK[u]
            return ps[:, b:b + 2, :].rearrange("p b (h t k) -> p (b h) t k", h=2, t=2)

        def bank(b, n):
            return ps[:, b, 0:n]

        def slots(x, i, part):
            return x[:, :, part:4:2, :] if i == 0 else x[:, :, 2 * part:2 * part + 2, :]

        def x_of(at):
            b = at.sequence if at.peeled else bass.ds(at.sequence, 1)
            rows = xs[:, b, at.j, :]
            return rows if at.peeled else rows.rearrange("p b d -> p (b d)")

        def heads_twice(x):
            return x.rearrange("p (h d) -> p h d", h=NH).unsqueeze(2).to_broadcast([P, NH, 2, HD])

        block = ctx.enter_context(nc.Block())

        @block.sync
        def _(sp):
            sp.dma_start(c_s[:, :, :], c_t.rearrange("(k p) b -> p k b", p=P)).then_inc(ld_c, 16)
            sp.dma_start(xs[:, 0, 0, :], x_t[0]).then_inc(ld_x[0], 16)
            sp.dma_start(wqkv_s[:, :, :], wqkv.rearrange("(k p) n -> p k n", p=P)).then_inc(ld_w, 16)
            sp.dma_start(xs[:, 0, 1:JT, :], x_t[1:JT].rearrange("j p d -> p j d")).then_inc(ld_x[1], 16)
            sp.dma_start(wo_s[:, :, :], wo.rearrange("(k p) n -> p k n", p=P)).then_inc(ld_w, 16)
            sp.dma_start(gate_s[:, :, :], gate_t.rearrange("(k p) n -> p k n", p=P)).then_inc(ld_w, 16)
            sp.dma_start(up_s[:, :, :], up_t.rearrange("(k p) n -> p k n", p=P)).then_inc(ld_w, 16)
            sp.dma_start(down_s[:, :, :], down.rearrange("(k p) n -> p k n", p=P)).then_inc(ld_w, 16)
            for b in range(1, BATCH):
                sp.dma_start(xs[:, b, :, :], x_t[JT * b:JT * (b + 1)].rearrange("j p d -> p j d")).then_inc(ld_x[2], 16)

            def slot(seq, r, live):
                g = At(seq, r - 3)
                if "G" in live:
                    wait(sp, g_out, g.count(1, 1))
                    sp.dma_start(out_t[g.index], obuf[:, g.k % 2, :]).then_inc(st_out[g.k % 2], 16)

            run_slots(sp, slot)
            for i in range(2):
                sp.wait_ge(st_out[i], 16 * TILES // 2)

        @block.tensor
        def _(pe):
            def transposes(dst, srcs, done):
                for i, src in enumerate(srcs):
                    last = pe.transpose(dst[:, i * P:(i + 1) * P], src, ident[:, :])
                last.then_inc(done, 1)

            def project(dst, lhs_t, rhs, parts, done):
                for k in range(parts):
                    last = pe.matmul(dst, lhs_t(k), rhs(k), start=(k == 0), stop=(k == parts - 1))
                last.then_inc(done, 1)

            pe.wait_ge(ld_mod, 16)
            pe.wait_ge(m_silu, 1)
            for i, m in enumerate((0, 1, 3, 4)):
                for h in range(DC):
                    for k in range(DC):
                        o = (i * DC + h) * BATCH
                        last = pe.matmul(ps[:, 0, o:o + BATCH], wmod_s[:, k, m * D + h * P:m * D + (h + 1) * P],
                                         silu[:, k, :], start=(k == 0), stop=(k == DC - 1))
            last.then_inc(m_cols, 1)
            pe.wait_ge(c_ident, 2)

            def gate_rows():
                pe.wait_ge(m_silu, 2)
                for b in range(BATCH):
                    if b > 1:
                        pe.wait_ge(m_rows_s, b - 1)
                    for k in range(DC):
                        last = pe.matmul(ps[:, PT_BANK[b % 2], :], silu_rows[:, k, b, :],
                                         wmod_s[:, k, :].rearrange("p (a m n) -> p a m n", a=2, m=3)[:, :, 2, :],
                                         start=(k == 0), stop=(k == DC - 1))
                    last.then_inc(m_rows, 1)

            def scores(t, c):
                u = c % 2
                wait(pe, v_sub, t.count(NC, c - 1))
                wait(pe, a_q, t.count(2, 1 + c // 2))
                wait(pe, a_k, t.count(4, 2 + 2 * (c // 2)))
                if t.peeled and t.index == 0:
                    pe.wait_ge(c_half, 1)
                for i in range(2):
                    g = 2 * c + i
                    dst = ps[:, S_BANK[u] + i, :].rearrange("p (h n) -> p h n", h=2)
                    if t.j == 0:
                        dst, keys = dst[:, :, P:2 * P], kT[:, g, :, 0, :]
                    else:
                        keys = kT[:, g, :, t.j - 1:t.j + 1, :].rearrange("p h t k -> p h (t k)")
                    last = pe.matmul(dst, qT[:, g, :], keys, start=True, stop=True)
                last.then_inc(p_s, 1)

            def scores_T(t, c):
                wait(pe, a_oT, t.count(NC, c - 1))
                if t.peeled and t.index == 0 and c < 2:
                    pe.wait_ge(m_rows_s, BATCH)
                wait(pe, v_sub, t.count(NC, c + 1))
                transposes(ps[:, PT_BANK[c % 2], :], [shifted[:, c % 2, i, :] for i in range(CH)], p_sT)

            def values(t, c):
                wait(pe, a_v, t.count(1, 1))
                wait(pe, g_sel, t.count(NC, c + 1))
                if t.j > 0:
                    for i in range(CH):
                        pe.matmul(ps[32 * i:32 * i + VW, PT_BANK[c % 2], 0:P], v_s[:, t.j - 1, CH * c + i, :],
                                  prev_p[:, c % 2, i, :], start=True, stop=False)
                for i in range(CH):
                    last = pe.matmul(ps[32 * i:32 * i + VW, PT_BANK[c % 2], 0:P], v_s[:, t.j, CH * c + i, :],
                                     own_p[:, c % 2, i, :], start=(t.j == 0), stop=True)
                last.then_inc(p_pv, 1)

            def qk_T(p, i, n):
                wait(pe, a_hi, p.count(2, 2))
                wait(pe, v_lo, p.count(2, 2))
                srcs = []
                for g in range(CH * n, CH * n + CH):
                    pair = hilo[:, i, 2 * g:2 * g + 2, :, :].bitcast(F32)
                    srcs.append(pair.rearrange("p h s d -> p (h s d)"))
                transposes(ps[:, W6 if (i, n) == (0, 1) else W7, :], srcs, p_kq)

            def x_T(l):
                wait(pe, v_xn, l.count(1, 1))
                transposes(ps[:, W6, :], [xn[:, k * P:(k + 1) * P] for k in range(DC)], p_xT)

            def queries_keys(x):
                if x.peeled and x.index == 0:
                    pe.wait_ge(ld_w, 16 * W_DMAS)
                wait(pe, a_hT, x.count(1, 1))
                wait(pe, a_q, x.count(2, -2))
                project(ps[:, W6, :], lambda k: hT[:, k, :], lambda k: wqkv_s[:, k, 0:2 * D], DC, p_qk)

            def values_of(x):
                wait(pe, a_qk, x.count(1, 1))
                project(ps[:, W6, 0:D], lambda k: hT[:, k, :], lambda k: wqkv_s[:, k, 2 * D:3 * D], DC, p_v)

            def slot(seq, r, live):
                l, x, p, t, f, g = (At(seq, r - lag) for lag in range(-2, 4))
                if "F" in live:
                    values(f, 2)
                    values(f, 3)
                if "T" in live:
                    wait(pe, *((a_z, g.count(1, 0)) if not g.peeled or g.index > 0 else (a_hT, x.count(1, 1))))
                    qk_T(t, 0, 1)
                if "G" in live:
                    wait(pe, *((a_k, t.count(4, 4)) if "T" in live else (v_hm, g.count(1, 0))))
                    wait(pe, v_xn2, g.count(1, 1))
                    transposes(ps[:, W7, :], [xn2[:, k * P:(k + 1) * P] for k in range(DC)], p_h2T)
                if "X" in live:
                    queries_keys(x)
                if "G" in live:
                    wait(pe, a_h2T, g.count(1, 1))
                    project(ps[:, W7, 0:EXPERTS], lambda k: h2T[:, k, :], lambda k: gate_s[:, k, :], DC, p_lg)
                if "T" in live:
                    scores_T(t, 0)
                    scores_T(t, 1)
                    scores(t, 2)
                    scores(t, 3)
                if "X" in live:
                    values_of(x)
                if "G" in live:
                    wait(pe, a_lg, g.count(1, 1))
                    wait(pe, v_onehot, g.count(1, 1))
                    for i in range(EC):
                        chosen = onehot[:, :, :].rearrange("p e r -> p (e r)")[:, i * P:(i + 1) * P]
                        last = pe.matmul(ps[:, W7, i * P:(i + 1) * P], chosen, ident_b[:, :], start=True, stop=True)
                    last.then_inc(p_mask, 1)
                if "F" in live:
                    wait(pe, *((a_v, x.count(1, 1)) if "X" in live else
                               (a_q, t.count(2, 2)) if "T" in live else (a_z, g.count(1, 0))))
                    wait(pe, a_oT, f.count(NC, NC))
                    transposes(ps[:, W6, :], [oT[:, i, :] for i in range(NC)], p_o)
                if "G" in live:
                    wait(pe, a_mask, g.count(1, 1))
                    for i in range(EC):
                        for k in range(DC):
                            last = pe.matmul(ps[:, W7, i * P:(i + 1) * P], up_s[:, k, i * P:(i + 1) * P],
                                             h2T[:, k, :], start=(k == 0), stop=(k == DC - 1))
                    last.then_inc(p_up, 1)
                if "F" in live:
                    wait(pe, v_on, f.count(1, 1))
                    flat = on[:, :, :].rearrange("p h d -> p (h d)")
                    transposes(ps[:, W6, :], [flat[:, k * P:(k + 1) * P] for k in range(DC)], p_onT)
                if "T" in live:
                    values(t, 0)
                    values(t, 1)
                if "P" in live:
                    wait(pe, *((v_hm, g.count(1, 1)) if "G" in live else (a_k, p.count(4, 0))))
                    qk_T(p, 1, 0)
                if "F" in live:
                    wait(pe, a_onT, f.count(1, 1))
                    project(ps[:, W6, 0:D], lambda k: onT[:, k, :], lambda k: wo_s[:, k, :], DC, p_wo)
                if "P" in live:
                    wait(pe, a_k, p.count(4, 2))
                    qk_T(p, 0, 0)
                if "L" in live:
                    wait(pe, *((a_y, f.count(1, 1)) if "F" in live else (a_v, x.count(1, 1))))
                    x_T(l)
                if "T" in live:
                    scores_T(t, 2)
                    scores_T(t, 3)
                if "P" in live:
                    scores(p, 0)
                    scores(p, 1)
                    wait(pe, a_q, p.count(2, 1))
                    qk_T(p, 1, 1)
                if "G" in live:
                    wait(pe, *((a_hT, l.count(1, 1)) if "L" in live else
                               (a_y, f.count(1, 1)) if "F" in live else (a_z, g.count(1, 0))))
                    wait(pe, v_hm, g.count(1, 1))
                    project(ps[:, W6, 0:D], lambda k: hm[:, k, :], lambda k: down_s[:, k, :], EC, p_down)
                if p.peeled and p.index == 0:
                    gate_rows()

            x_T(At(0, 0))
            queries_keys(At(0, 0))
            values_of(At(0, 0))
            pe.wait_ge(a_v, 1)
            x_T(At(0, 1))
            run_slots(pe, slot)

        @block.scalar
        def _(act):
            target = act.alloc_register("act_target")
            act.dma_start(wmod_s[:, :, :], wmod.rearrange("(k p) n -> p k n", p=P)).then_inc(ld_mod, 16)
            act.dma_start(trig_s[:, :, :, :, :], trig.rearrange("(j p) a b d -> p j a b d", p=P)).then_inc(ld_trig, 16)
            act.dma_start(normw[:, 0, :], qw.partition_broadcast(P)).then_inc(ld_trig, 16)
            act.dma_start(normw[:, 1, :], kw.partition_broadcast(P)).then_inc(ld_trig, 16)
            act.wait_ge(ld_c, 16)
            act.activation(ec[:, :, :], c_s[:, :, :], ACT.Exp, scale=-1.0).then_inc(m_exp, 1)
            act.wait_ge(m_cols, 1)
            act.activation(mod_s[:, :, :, :].rearrange("p m h b -> p (m h b)"), ps[:, 0, 0:4 * DC * BATCH],
                           ACT.Identity).then_inc(m_cols_s, 1)
            act.wait_ge(m_mod, 1)

            def modulate(dst, b_ps, which, at, done):
                b = at.sequence
                for h in range(DC):
                    last = act.activation(dst[:, h, :], ps[:, b_ps, h * P:(h + 1) * P], ACT.Identity,
                                          scale=mod_s[:, 2 * which + 1, h, bass.ds(b, 1)],
                                          bias=mod_s[:, 2 * which, h, bass.ds(b, 1)])
                last.then_inc(done, 1)

            def hidden(l):
                wait(act, p_v, l.count(1, 0))
                wait_alone(act, p_xT, l.count(1, 1), target, m_mod)
                modulate(hT, W6, 0, l, a_hT)

            def queries_keys(x):
                wait(act, g_rot, x.count(3, 0))
                wait(act, a_ssq, x.count(2, 0))
                wait(act, p_qk, x.count(1, 1))
                act.activation(qk[:, :, :].rearrange("p a d -> p (a d)"), ps[:, W6, :],
                               ACT.Identity).then_inc(a_qk, 1)

            def squares(x):
                wait(act, a_qk, x.count(1, 1))
                wait(act, v_ssqe, x.count(1, 0))
                for i in range(2):
                    wait(act, a_ssq, x.count(2, i))
                    act.activation(sq[:, :], qk[:, i, :], ACT.Square, accum_out=ssq[:, i:i + 1]).then_inc(a_ssq, 1)

            def values_of(x):
                wait(act, p_pv, x.count(NC, -2 * NC))
                if x.peeled and x.index == 0:
                    act.wait_ge(c_ones, 1)
                wait(act, p_v, x.count(1, 1))
                act.activation(v_s[:, x.j, :, 0:HD], ps[:, W6, 0:D].rearrange("p (h d) -> p h d", h=NH),
                               ACT.Identity).then_inc(a_v, 1)

            def slot(seq, r, live):
                l, x, p, t, f, g = (At(seq, r - lag) for lag in range(-2, 4))

                def exps(c):
                    wait(act, g_sel, t.count(NC, c - 1))
                    wait(act, p_sT, t.count(NC, c + 1))
                    act.activation(expT[:, c % 2, :, :].rearrange("p h q -> p (h q)"), ps[:, PT_BANK[c % 2], :],
                                   ACT.Exp).then_inc(a_exp, 1)

                def out_T(t, c):
                    wait(act, p_o, t.count(1, 0))
                    wait(act, p_pv, t.count(NC, c + 1))
                    act.activation(oT[:, c, :], ps[:, PT_BANK[c % 2], 0:P], ACT.Identity).then_inc(a_oT, 1)

                def k_rows(n):
                    wait(act, p_s, p.count(NC, -2 * NC))
                    wait(act, p_kq, p.count(4, 2 * n + 1))
                    for h in range(2):
                        act.activation(kT[64 * h:64 * h + 64, CH * n:CH * n + CH, h, p.j, :],
                                       ps[64 * h:64 * h + 64, W7, :].rearrange("p (g k) -> p g k", g=CH),
                                       ACT.Identity).then_inc(a_k, 1)

                def q_rows(p, n):
                    wait(act, p_s, p.count(NC, 0))
                    wait(act, p_kq, p.count(4, 2 * n + 2))
                    act.activation(qT[:, CH * n:CH * n + CH, :].rearrange("p g k -> p (g k)"), ps[:, W6 if n else W7, :],
                                   ACT.Identity).then_inc(a_q, 1)

                if "F" in live:
                    out_T(f, 2)
                    out_T(f, 3)
                if "T" in live:
                    q_rows(t, 1)
                if "G" in live:
                    wait(act, p_up, g.count(1, 0))
                    wait_alone(act, p_h2T, g.count(1, 1), target, m_mod)
                    modulate(h2T, W7, 1, g, a_h2T)
                if "P" in live:
                    wait(act, p_kq, p.count(4, 0))
                    wait(act, g_rqk, p.count(1, 1))
                    wait(act, v_rot, p.count(1, 1))
                    for i in (1, 0):
                        act.activation(slots(hilo[:, i, :, :, :], i, 0), heads_twice(rot[:, i, :]), ACT.Identity,
                                       scale=rqk[:, i:i + 1]).then_inc(a_hi, 1)
                if "G" in live:
                    wait(act, v_onehot, g.count(1, 0))
                    wait(act, p_lg, g.count(1, 1))
                    act.activation(lgs[:, :], ps[:, W7, 0:EXPERTS], ACT.Identity).then_inc(a_lg, 1)
                if "X" in live:
                    queries_keys(x)
                if "T" in live:
                    exps(0)
                    exps(1)
                if "G" in live:
                    wait(act, v_psel, g.count(1, 0))
                    wait(act, v_gate, g.count(4, 1))
                    act.activation(lexp[:, :], lgs[:, :], ACT.Exp, bias=nmx[:, :], accum_out=lsum[:, :]).then_inc(a_lsum, 1)
                if "X" in live:
                    squares(x)
                    values_of(x)
                if "G" in live:
                    wait(act, v_hm, g.count(1, 0))
                    wait(act, p_mask, g.count(1, 1))
                    act.activation(maskT[:, :, :].rearrange("p e t -> p (e t)"), ps[:, W7, :],
                                   ACT.Identity).then_inc(a_mask, 1)
                if "F" in live:
                    wait(act, p_wo, f.count(1, 0))
                    wait(act, p_onT, f.count(1, 1))
                    act.activation(onT[:, :, :].rearrange("p k t -> p (k t)"), ps[:, W6, 0:D],
                                   ACT.Identity).then_inc(a_onT, 1)
                if "T" in live:
                    out_T(t, 0)
                    out_T(t, 1)
                if "P" in live:
                    k_rows(0)
                if "F" in live:
                    wait(act, g_yg, f.count(1, 0))
                    wait(act, p_wo, f.count(1, 1))
                    act.activation(y[:, :], ps[:, W6, 0:D], ACT.Identity).then_inc(a_y, 1)
                if "P" in live:
                    q_rows(p, 0)
                if "L" in live:
                    hidden(l)
                if "T" in live:
                    exps(2)
                    exps(3)
                if "P" in live:
                    k_rows(1)
                if "G" in live:
                    wait(act, g_zg, g.count(1, 0))
                    wait(act, v_psel, g.count(1, 1))
                    wait(act, p_down, g.count(1, 1))
                    act.activation(z[:, :], ps[:, W6, 0:D], ACT.Identity, scale=psel[:, :]).then_inc(a_z, 1)
                if p.peeled and p.index == 0:
                    for b in range(BATCH):
                        act.wait_ge(m_rows, b + 1)
                        act.activation(gates[:, b, :, :].rearrange("p a n -> p (a n)"), ps[:, PT_BANK[b % 2], :],
                                       ACT.Identity).then_inc(m_rows_s, 1)

            hidden(At(0, 0))
            queries_keys(At(0, 0))
            squares(At(0, 0))
            values_of(At(0, 0))
            hidden(At(0, 1))
            run_slots(act, slot)

        @block.vector
        def _(dve):
            target = dve.alloc_register("dve_target")
            dve.memset(kT[0:64, :, 1, :, :].bitcast(F32), 0.0).then_inc(c_zero, 1)
            dve.wait_ge(m_exp, 1)
            dve.tensor_scalar(ec1[:, :, :], ec[:, :, :], 1.0, None, ALU.add).then_inc(m_dve, 1)
            dve.wait_ge(m_dve, 1)
            dve.reciprocal(sig[:, :, :], ec1[:, :, :]).then_inc(m_dve, 1)
            dve.wait_ge(m_dve, 2)
            dve.tensor_tensor(silu[:, :, :], c_s[:, :, :], sig[:, :, :], ALU.mult).then_inc(m_silu, 1)
            dve.wait_ge(m_silu, 1)
            dve.tensor_copy(silu_rows[:, :, :, :], silu[:, :, :].unsqueeze(3).to_broadcast([P, DC, BATCH, P])).then_inc(m_silu, 1)

            def stats(src, st, mv, ve, s_st, s_ve, at):
                dve.bn_stats(out=st[:, :], in_=src).then_inc(s_st, 1)
                wait_alone(dve, s_st, at.count(2, 1), target, c_zero)
                dve.bn_aggr(out=mv[:, :], in_=st[:, :]).then_inc(s_st, 1)
                wait(dve, s_st, at.count(2, 2))
                dve.tensor_scalar(ve[:, :], mv[:, 1:2], EPS_LN, None, ALU.add).then_inc(s_ve, 1)

            def normed(dst, src, mv, rs, done):
                dve.tensor_scalar(dst[:, :], src, mv[:, 0:1], rs[:, 0:1], ALU.subtract, ALU.mult).then_inc(done, 1)

            def ln1_stats(at):
                if at.peeled and at.index in (0, 1, JT):
                    part = (0, 1, JT).index(at.index)
                    dve.wait_ge(ld_x[part], 16 if part < 2 else 16 * (BATCH - 1))
                wait(dve, g_rs1, at.count(1, 0))
                stats(x_of(at), st1, mv1, ve1, v_st1, v_ve1, at)

            def ln1(at):
                wait(dve, p_xT, at.count(1, 0))
                wait(dve, g_rs1, at.count(1, 1))
                normed(xn, x_of(at), mv1, rs1, v_xn)

            ln1_stats(At(0, 0))
            dve.wait_ge(c_pool, 1)
            dve.tensor_copy(take_prev[:, :], take_f[:, :]).then_inc(c_pick, 1)
            dve.wait_ge(m_cols_s, 1)
            dve.tensor_scalar(mod_s[:, 1:4:2, :, :], mod_s[:, 1:4:2, :, :], 1.0, None, ALU.add).then_inc(m_mod, 1)
            ln1(At(0, 0))
            dve.wait_ge(ld_trig, 48)
            for i in range(2):
                w = normw[:, i, :].rearrange("p (h d) -> p h d", h=NH)
                dve.tensor_tensor(cosw[:, :, i, :].rearrange("p j (h d) -> p j h d", h=NH),
                                  w.unsqueeze(1).to_broadcast([P, JT, NH, HD]),
                                  trig_s[:, :, i, 0, :].unsqueeze(2).to_broadcast([P, JT, NH, HD]),
                                  ALU.mult).then_inc(c_rope, 1)
                for a in range(2):
                    dve.tensor_tensor(
                        sinw[:, :, i, :].rearrange("p j (h a d) -> p j h a d", h=NH, a=2)[:, :, :, a, :],
                        w[:, :, HALF * (1 - a):HALF * (2 - a)].unsqueeze(1).to_broadcast([P, JT, NH, HALF]),
                        trig_s[:, :, i, 1, HALF * a:HALF * (a + 1)].unsqueeze(2).to_broadcast([P, JT, NH, HALF]),
                        ALU.mult).then_inc(c_rope, 1)

            def mean_squares(x):
                wait(dve, g_rqk, x.count(1, 0))
                wait(dve, a_ssq, x.count(2, 2))
                dve.tensor_scalar(ssqe[:, :], ssq[:, :], 1.0 / D, EPS_RMS, ALU.mult, ALU.add).then_inc(v_ssqe, 1)

            def rotated(x):
                flat = [x.rearrange("p a d -> p (a d)") for x in (rot[:, :, :], t1[:, :, :], t2[:, :, :])]
                wait(dve, a_hi, x.count(2, 0))
                wait(dve, g_rot, x.count(3, 3))
                dve.tensor_tensor(*flat, ALU.add).then_inc(v_rot, 1)
                wait(dve, v_rot, x.count(1, 1))
                wait(dve, g_rqk, x.count(1, 1))
                for i in range(2):
                    dve.tensor_scalar(rr[:, i, :], rot[:, i, :], rqk[:, i:i + 1], None, ALU.mult).then_inc(v_rr, 1)

            def gate_values():
                n = 0
                for b in range(BATCH):
                    raw = gates[:, b, :, :].rearrange("p a n -> p (a n)")
                    dve.wait_ge(m_rows_s, b + 1)
                    if b:
                        dve.wait_ge(m_gates, b)
                    dve.tensor_scalar(gsgn[:, :], raw, 0.0, 2.0, ALU.is_ge, ALU.mult).then_inc(m_gdve, 1)
                    dve.scalar_tensor_tensor(out=gtmp[:, :], in0=raw, scalar=-1.0, in1=raw, op0=ALU.mult,
                                             op1=ALU.max).then_inc(m_gdve, 1)
                    n += 2
                    dve.wait_ge(m_gdve, n)
                    dve.tensor_scalar(gtmp[:, 0:D], gtmp[:, 0:D], 0.25, None, ALU.max).then_inc(m_gdve, 1)
                    dve.tensor_scalar(gtmp[:, D:2 * D], gtmp[:, D:2 * D], 0.25, SCALING, ALU.max,
                                      ALU.mult).then_inc(m_gdve, 1)
                    n += 2
                    dve.wait_ge(m_gdve, n)
                    dve.scalar_tensor_tensor(out=raw, in0=gsgn[:, :], scalar=-1.0, in1=gtmp[:, :], op0=ALU.add,
                                             op1=ALU.mult).then_inc(m_gates, 1)

            def slot(seq, r, live):
                l, x, p, t, f, g = (At(seq, r - lag) for lag in range(-2, 4))

                def own(c):
                    return scores_of(c % 2)[:, :, 1, :]

                def merge(c):
                    pick = take_prev[:, :].unsqueeze(1).to_broadcast([P, CH, P])
                    other = (scores_of(c % 2)[:, :, 0, :] if t.j else
                             neg_s[:, :].unsqueeze(1).to_broadcast([P, CH, P]))
                    if t.peeled and t.index == 0:
                        dve.wait_ge(c_pick, 1)
                        dve.wait_ge(c_ones, 1)
                    wait_alone(dve, p_s, t.count(NC, c + 1), target, c_zero)
                    dve.copy_predicated(own(c), pick, other).then_inc(v_pick, 1)

                def maximum(c):
                    wait(dve, v_pick, t.count(NC, c + 1))
                    dve.tensor_reduce(negm[:, c % 2, :], own(c), AX.X, ALU.max, negate=True).then_inc(v_max, 1)

                def subtract(c):
                    wait(dve, p_sT, t.count(NC, c - 1))
                    wait(dve, v_max, t.count(NC, c + 1))
                    dve.tensor_tensor(shifted[:, c % 2, :, :], own(c),
                                      negm[:, c % 2, :].unsqueeze(2).to_broadcast([P, CH, P]),
                                      ALU.add).then_inc(v_sub, 1)

                def lo(i, n):
                    if n == 0:
                        wait(dve, v_rr, p.count(2, 2))
                        wait(dve, p_kq, p.count(4, 0))
                    wait(dve, a_hi, p.count(2, 1 + n))
                    dve.tensor_tensor(slots(hilo[:, i, :, :, :], i, 1), heads_twice(rr[:, i, :]),
                                      slots(hilo[:, i, :, :, :], i, 0).bitcast(F32), ALU.subtract).then_inc(v_lo, 1)

                if "T" in live:
                    merge(0)
                    merge(1)
                if "G" in live:
                    wait(dve, p_h2T, g.count(1, 0))
                    wait(dve, g_rs2, g.count(1, 1))
                    normed(xn2, x1[:, g.k % 2, :], mv2, rs2, v_xn2)
                if "T" in live:
                    maximum(0)
                    maximum(1)
                    subtract(0)
                    subtract(1)
                if "P" in live:
                    lo(1, 0)
                if "G" in live:
                    wait(dve, a_lsum, g.count(1, 0))
                    wait(dve, a_lg, g.count(1, 1))
                    dve.tensor_reduce(nmx[:, :], lgs[:, :], AX.X, ALU.max, negate=True).then_inc(v_gate, 1)
                if "P" in live:
                    lo(0, 1)
                if "G" in live:
                    wait(dve, v_gate, g.count(4, 1))
                    dve.tensor_scalar(ge[:, :], lgs[:, :], nmx[:, :], 0.0, ALU.add, ALU.is_ge).then_inc(v_gate, 1)
                    wait(dve, v_gate, g.count(4, 2))
                    dve.tensor_tensor(score[:, :], ge[:, :], first_s[:, :], ALU.mult).then_inc(v_gate, 1)
                    wait(dve, v_gate, g.count(4, 3))
                    dve.tensor_reduce(best[:, :], score[:, :], AX.X, ALU.max).then_inc(v_gate, 1)
                    wait(dve, a_z, g.count(1, 0))
                    wait(dve, a_lsum, g.count(1, 1))
                    dve.reciprocal(psel[:, :], lsum[:, :]).then_inc(v_psel, 1)
                    wait(dve, p_mask, g.count(1, 0))
                    wait(dve, v_gate, g.count(4, 4))
                    dve.tensor_scalar(onehot[:, :, :], score[:, :].unsqueeze(2).to_broadcast([P, EXPERTS, RANK]),
                                      best[:, :], None, ALU.is_equal).then_inc(v_onehot, 1)
                if "L" in live:
                    ln1_stats(l)
                if "T" in live:
                    merge(2)
                    merge(3)
                if "X" in live:
                    mean_squares(x)
                if "F" in live:
                    heads = ps[:, W6, :].rearrange("p (h d) -> p h d", h=NH)
                    wait(dve, p_o, f.count(1, 1))
                    dve.reciprocal(rden[:, :], heads[:, :, HD]).then_inc(v_rden, 1)
                    wait(dve, v_rden, f.count(1, 1))
                    wait(dve, p_onT, f.count(1, 0))
                    dve.tensor_tensor(on[:, :, :], heads[:, :, 0:HD],
                                      rden[:, :].unsqueeze(2).to_broadcast([P, NH, HD]), ALU.mult).then_inc(v_on, 1)
                if "G" in live:
                    wait(dve, a_mask, g.count(1, 1))
                    wait(dve, p_down, g.count(1, 0))
                    wait(dve, p_up, g.count(1, 1))
                    dve.tensor_tensor(hm[:, :, :].rearrange("p e t -> p (e t)"), ps[:, W7, :],
                                      maskT[:, :, :].rearrange("p e t -> p (e t)"), ALU.mult).then_inc(v_hm, 1)
                if "L" in live:
                    ln1(l)
                if "T" in live:
                    maximum(2)
                    maximum(3)
                    subtract(2)
                    subtract(3)
                if "X" in live:
                    rotated(x)
                if "F" in live:
                    wait(dve, g_rs2, f.count(1, 0))
                    wait(dve, g_x1, f.count(1, 1))
                    stats(x1[:, f.k % 2, :], st2, mv2, ve2, v_st2, v_ve2, f)
                if p.peeled and p.index == 1:
                    gate_values()

            ln1_stats(At(0, 1))
            ln1(At(0, 1))
            mean_squares(At(0, 0))
            rotated(At(0, 0))
            run_slots(dve, slot)

        @block.gpsimd
        def _(pool):
            target = pool.alloc_register("pool_target")
            pool.memset(ones_f[:, :], 1.0).then_inc(c_const, 1)
            pool.memset(pow_s[:, :], -0.5).then_inc(c_const, 1)
            pool.wait_ge(c_const, 2)
            pool.affine_select(out=ident[:, :], in_=ones_f[:, :], compare_op=ALU.is_equal, fill=0.0, base=0,
                               pattern=[[1, P]], channel_multiplier=-1).then_inc(c_ident, 1)
            pool.affine_select(out=ident_b[:, :], in_=ones_f[:, :], compare_op=ALU.is_equal, fill=0.0, base=0,
                               pattern=[[1, P]], channel_multiplier=-1).then_inc(c_ident, 1)
            pool.affine_select(out=take_f[:, :], in_=ones_f[:, :], compare_op=ALU.is_ge, fill=0.0, base=-1,
                               pattern=[[1, P]], channel_multiplier=-1).then_inc(c_pool, 1)
            pool.wait_ge(v_ve1, 1)
            pool.tensor_tensor(rs1[:, :], ve1[:, :], pow_s[:, 0:1], ALU.pow).then_inc(g_rs1, 1)
            pool.memset(neg_s[:, :], NEG)
            for e in range(EXPERTS):
                pool.memset(first_s[:, e:e + 1], float(EXPERTS - e))
            pool.memset(v_s[:, :, :, HD:VW], 1.0).then_inc(c_ones, 1)
            pool.wait_ge(c_ones, 1)
            pool.memset(kT[64:128, :, 0, :, :].bitcast(F32), 0.0).then_inc(c_half, 1)
            pool.wait_ge(c_half, 1)

            def rotate(x):
                wait(pool, v_rot, x.count(1, 0))
                if x.peeled and x.index == 0:
                    pool.wait_ge(c_rope, 6)
                wait(pool, a_qk, x.count(1, 1))
                pool.tensor_tensor(t1[:, :, :], qk[:, :, :], cosw[:, x.j, :, :], ALU.mult).then_inc(g_rot, 1)
                halves = [x.rearrange("p i (h a d) -> p (i h) a d", h=NH, a=2)
                          for x in (t2[:, :, :], qk[:, :, :], sinw[:, x.j, :, :])]
                for a in range(2):
                    pool.tensor_tensor(halves[0][:, :, a, :], halves[1][:, :, 1 - a, :], halves[2][:, :, a, :],
                                       ALU.mult).then_inc(g_rot, 1)
                wait(pool, v_rr, x.count(2, 0))
                wait(pool, a_hi, x.count(2, 0))
                wait(pool, v_ssqe, x.count(1, 1))
                pool.tensor_tensor(rqk[:, :], ssqe[:, :], pow_s[:, :], ALU.pow).then_inc(g_rqk, 1)

            def slot(seq, r, live):
                l, x, p, t, f, g = (At(seq, r - lag) for lag in range(-2, 4))

                def select(t, c):
                    u = c % 2
                    wait_alone(pool, a_exp, t.count(NC, c + 1), target, c_const)
                    if t.j:
                        pool.affine_select(out=prev_p[:, u, :, :], in_=expT[:, u, :, :], compare_op=ALU.is_ge,
                                           fill=0.0, base=-1, pattern=[[0, CH], [-1, P]], channel_multiplier=1)
                    pool.affine_select(out=own_p[:, u, :, :], in_=expT[:, u, :, :], compare_op=ALU.is_ge,
                                       fill=0.0, base=0, pattern=[[0, CH], [1, P]],
                                       channel_multiplier=-1).then_inc(g_sel, 1)

                if "T" in live:
                    select(t, 0)
                    select(t, 1)
                if "L" in live:
                    wait(pool, v_xn, l.count(1, 0))
                    wait(pool, v_ve1, l.count(1, 1))
                    pool.tensor_tensor(rs1[:, :], ve1[:, :], pow_s[:, 0:1], ALU.pow).then_inc(g_rs1, 1)
                if "X" in live:
                    rotate(x)
                if "F" in live:
                    if f.peeled and f.index == 0:
                        pool.wait_ge(m_gates, BATCH)
                    wait_alone(pool, a_y, f.count(1, 1), target, c_const)
                    pool.tensor_tensor(yg[:, :], y[:, :], gates[:, f.sequence, 0, :], ALU.mult).then_inc(g_yg, 1)
                    wait(pool, g_out, f.count(1, -1))
                    wait(pool, g_yg, f.count(1, 1))
                    pool.tensor_tensor(x1[:, f.k % 2, :], x_of(f), yg[:, :], ALU.add).then_inc(g_x1, 1)
                if "T" in live:
                    select(t, 2)
                    select(t, 3)
                if "F" in live:
                    wait(pool, v_xn2, f.count(1, 0))
                    wait(pool, v_ve2, f.count(1, 1))
                    pool.tensor_tensor(rs2[:, :], ve2[:, :], pow_s[:, 0:1], ALU.pow).then_inc(g_rs2, 1)
                if "G" in live:
                    if "F" not in live:
                        pool.wait_ge(g_out, TILES - 1)
                    wait_alone(pool, a_z, g.count(1, 1), target, c_const)
                    pool.tensor_tensor(zg[:, :], z[:, :], gates[:, g.sequence, 1, :], ALU.mult).then_inc(g_zg, 1)
                if "G" in live:
                    if g.peeled:
                        n = 16 * (g.index // 2)
                        wait(pool, st_out[g.k % 2], n if n else None)
                    else:
                        pool.wait_ge(st_out[g.k % 2], seq * (16 * JT // 2) + 16 * (g.k // 2))
                    wait(pool, g_zg, g.count(1, 1))
                    pool.tensor_tensor(obuf[:, g.k % 2, :], x1[:, g.k % 2, :], zg[:, :], ALU.add).then_inc(g_out, 1)

            pool.wait_ge(v_xn, 1)
            pool.wait_ge(v_ve1, 2)
            pool.tensor_tensor(rs1[:, :], ve1[:, :], pow_s[:, 0:1], ALU.pow).then_inc(g_rs1, 1)
            rotate(At(0, 0))
            run_slots(pool, slot)


def rotation_tables():
    inv = (1.0 / np.float32(10000.0) ** (np.arange(0, HD, 2, dtype=np.float32) / np.float32(HD))).astype(np.float32)
    angle = np.arange(SEQ, dtype=np.float32)[:, None] * inv[None, :]
    cos, sin = np.cos(angle).astype(np.float32), np.sin(angle).astype(np.float32)
    k = np.stack([np.concatenate([cos, cos], 1), np.concatenate([-sin, sin], 1)], 1)
    return np.ascontiguousarray(np.stack([k * np.float32(HD ** -0.5), k], 1))


def kernel(L0_attn_hidden_states, L0_attn_Wqkv, L0_attn_q_norm_w, L0_attn_k_norm_w, L0_attn_Wo, L0_ffn_A,
           L0_ffn_Bw, L0_ffn_Wg, L0_c, L0_wmod):
    import concourse.bacc as bacc
    from concourse.bass_utils import run_bass_kernel_spmd

    arrays = {
        "x": np.asarray(L0_attn_hidden_states).reshape(BATCH * SEQ, D),
        "c_t": np.asarray(L0_c).T,
        "wmod": np.asarray(L0_wmod),
        "wqkv": np.asarray(L0_attn_Wqkv),
        "qw": np.asarray(L0_attn_q_norm_w),
        "kw": np.asarray(L0_attn_k_norm_w),
        "wo": np.asarray(L0_attn_Wo),
        "up_t": np.asarray(L0_ffn_A).reshape(ER, D).T,
        "down": np.asarray(L0_ffn_Bw).transpose(0, 2, 1).reshape(ER, D),
        "gate_t": np.asarray(L0_ffn_Wg).T,
        "trig": rotation_tables(),
    }
    arrays = {n: np.ascontiguousarray(a) for n, a in arrays.items()}
    nc = bacc.Bacc("TRN2", target_bir_lowering=False, num_devices=1)
    ins = [nc.dram_tensor(n, a.shape, mybir.dt.from_np(a.dtype), kind="ExternalInput").ap() for n, a in arrays.items()]
    out = nc.dram_tensor("out", (BATCH * SEQ, D), F32, kind="ExternalOutput").ap()
    build(nc, *ins, out)
    r = run_bass_kernel_spmd(nc, [arrays], core_ids=[0])
    return r.results[0]["out"].reshape(BATCH, SEQ, D)
```

```python
from contextlib import ExitStack

import numpy as np
import concourse.bass as bass
from concourse import mybir

F32 = mybir.dt.float32
F32R = mybir.dt.float32r
BF16 = mybir.dt.bfloat16
U8 = mybir.dt.uint8
ALU = mybir.AluOpType
ACT = mybir.ActivationFunctionType
AX = mybir.AxisListType

P = 128
BATCH, SEQ, D = 4, 512, 256
NH, HD = 16, 16
HALF = HD // 2
JT = SEQ // P
TILES = BATCH * JT
DC = D // P
EXPERTS, RANK = 8, 64
ER = EXPERTS * RANK
EC = ER // P
CH = 4
NC = NH // CH
NG = NH // 2
VW = HD + 1
NEG = -1.0e30
EPS_RMS, EPS_LN = 1e-6, 1e-5
SCALING = 64.0 / 16.0

S_BANK = (0, 2)
PT_BANK = (4, 5)
W6, W7 = 6, 7


class At:

    def __init__(self, seq, k):
        self.seq, self.k = seq, k
        self.peeled = isinstance(seq, int)
        self.j = k % JT
        self.index = seq * JT + k
        self.sequence = seq + k // JT

    def count(self, per=1, extra=0):
        least = (self.seq if self.peeled else 1) * JT * per + self.k * per + extra
        if self.peeled:
            return least if least > 0 else None
        assert least > 0
        return self.seq * (JT * per) + (self.k * per + extra)


def wait(eng, sem, value):
    if value is not None:
        eng.wait_ge(sem, value)


def wait_alone(eng, sem, value, target, done):
    if value is None or isinstance(value, int):
        wait(eng, sem, value)
    else:
        eng.reg_mov(target, value)
        eng.wait_ge(done, 1)
        eng.wait_ge(sem, target)


STAGES = (("L", -2), ("X", -1), ("P", 0), ("T", 1), ("F", 2), ("G", 3))


def run_slots(eng, slot):
    def live(s):
        return {n for n, lag in STAGES if 0 <= s - lag < TILES}
    for r in range(JT):
        slot(0, r, live(r))
    with eng.Fori(1, BATCH - 1) as seq:
        for r in range(JT):
            slot(seq, r, live(JT + r))
    for r in range(JT + 3):
        slot(BATCH - 1, r, live(TILES - JT + r))


def build(nc, x, c_t, wmod, wqkv, qw, kw, wo, up_t, down, gate_t, trig, out):
    x_t = x.rearrange("(n p) d -> n p d", p=P)
    out_t = out.rearrange("(n p) d -> n p d", p=P)
    with ExitStack() as ctx:
        def sb(name, shape, dt=F32):
            return ctx.enter_context(nc.sbuf_tensor(name, shape, dt))

        def sem(name):
            return ctx.enter_context(nc.semaphore(name))

        ps = ctx.enter_context(nc.psum_tensor("ps", [P, 8, 512], F32))

        wqkv_s = sb("wqkv_s", [P, DC, 3 * D])
        wo_s = sb("wo_s", [P, DC, D])
        wmod_s = sb("wmod_s", [P, DC, 6 * D])
        up_s = sb("up_s", [P, DC, ER])
        down_s = sb("down_s", [P, EC, D])
        gate_s = sb("gate_s", [P, DC, EXPERTS])
        c_s = sb("c_s", [P, DC, BATCH])
        trig_s = sb("trig_s", [P, JT, 2, 2, HD])
        normw = sb("normw", [P, 2, D])
        ident = sb("ident", [P, P])
        ident_b = sb("ident_b", [P, P], BF16)
        ones_f = sb("ones_f", [P, P])
        take_prev = sb("take_prev", [P, P], U8)
        take_f = sb("take_f", [P, P])
        neg_s = sb("neg_s", [P, P])
        pow_s = sb("pow_s", [P, 2])
        first_s = sb("first_s", [P, EXPERTS])
        cosw = sb("cosw", [P, JT, 2, D])
        sinw = sb("sinw", [P, JT, 2, D])
        ec = sb("ec", [P, DC, BATCH])
        ec1 = sb("ec1", [P, DC, BATCH])
        sig = sb("sig", [P, DC, BATCH])
        silu = sb("silu", [P, DC, BATCH])
        silu_rows = sb("silu_rows", [P, DC, BATCH, P])
        mod_s = sb("mod_s", [P, 4, DC, BATCH])
        gates = sb("gates", [P, BATCH, 2, D])
        gtmp = sb("gtmp", [P, 2 * D])
        gsgn = sb("gsgn", [P, 2 * D])
        xs = sb("xs", [P, BATCH, JT, D])
        st1 = sb("st1", [P, 6])
        mv1 = sb("mv1", [P, 2])
        ve1 = sb("ve1", [P, 1])
        rs1 = sb("rs1", [P, 1])
        xn = sb("xn", [P, D])
        hT = sb("hT", [P, DC, P])
        qk = sb("qk", [P, 2, D])
        sq = sb("sq", [P, D])
        ssq = sb("ssq", [P, 2])
        ssqe = sb("ssqe", [P, 2])
        rqk = sb("rqk", [P, 2])
        t1 = sb("t1", [P, 2, D])
        t2 = sb("t2", [P, 2, D])
        rot = sb("rot", [P, 2, D])
        rr = sb("rr", [P, 2, D])
        hilo = sb("hilo", [P, 2, 2, NH, 4, HD], F32R)
        qT = sb("qT", [P, NG, P], F32R)
        kT = sb("kT", [P, NG, 2, JT, P], F32R)
        v_s = sb("v_s", [P, JT, NH, VW])
        negm = sb("negm", [P, 2, CH])
        shifted = sb("shifted", [P, 2, CH, P])
        expT = sb("expT", [P, 2, CH, P])
        own_p = sb("own_p", [P, 2, CH, P])
        prev_p = sb("prev_p", [P, 2, CH, P])
        oT = sb("oT", [P, NC, P])
        rden = sb("rden", [P, NH])
        on = sb("on", [P, NH, HD])
        onT = sb("onT", [P, DC, P])
        y = sb("y", [P, D])
        yg = sb("yg", [P, D])
        x1 = sb("x1", [P, 2, D])
        st2 = sb("st2", [P, 6])
        mv2 = sb("mv2", [P, 2])
        ve2 = sb("ve2", [P, 1])
        rs2 = sb("rs2", [P, 1])
        xn2 = sb("xn2", [P, D])
        h2T = sb("h2T", [P, DC, P])
        lgs = sb("lgs", [P, EXPERTS])
        nmx = sb("nmx", [P, 1])
        ge = sb("ge", [P, EXPERTS])
        score = sb("score", [P, EXPERTS])
        best = sb("best", [P, 1])
        onehot = sb("onehot", [P, EXPERTS, RANK], BF16)
        lexp = sb("lexp", [P, EXPERTS])
        lsum = sb("lsum", [P, 1])
        psel = sb("psel", [P, 1])
        maskT = sb("maskT", [P, EC, P], BF16)
        hm = sb("hm", [P, EC, P])
        z = sb("z", [P, D])
        zg = sb("zg", [P, D])
        obuf = sb("obuf", [P, D])

        ld_c, ld_mod, ld_trig, ld_wqkv, ld_w = (sem("ld_c"), sem("ld_mod"), sem("ld_trig"), sem("ld_wqkv"),
                                                sem("ld_w"))
        ld_x = [sem(f"ld_x{i}") for i in range(3)]
        st_out = sem("st_out")
        c_ident, c_zero, c_const, c_ones = sem("c_ident"), sem("c_zero"), sem("c_const"), sem("c_ones")
        c_pick, c_half = sem("c_pick"), sem("c_half")
        c_pool, c_rope = sem("c_pool"), sem("c_rope")
        m_exp, m_dve, m_silu, m_cols, m_cols_s = sem("m_exp"), sem("m_dve"), sem("m_silu"), sem("m_cols"), sem("m_cols_s")
        m_mod, m_rows, m_rows_s, m_gdve, m_gates = sem("m_mod"), sem("m_rows"), sem("m_rows_s"), sem("m_gdve"), sem("m_gates")
        p_xT, p_qk, p_v, p_kq = sem("p_xT"), sem("p_qk"), sem("p_v"), sem("p_kq")
        p_s, p_sT, p_pv = sem("p_s"), sem("p_sT"), sem("p_pv")
        p_o, p_onT, p_wo, p_h2T, p_lg = sem("p_o"), sem("p_onT"), sem("p_wo"), sem("p_h2T"), sem("p_lg")
        p_mask, p_up, p_down = sem("p_mask"), sem("p_up"), sem("p_down")
        a_hi, a_lg, a_y, a_z = sem("a_hi"), sem("a_lg"), sem("a_y"), sem("a_z")
        a_hT, a_qk, a_ssq, a_v, a_k, a_q = sem("a_hT"), sem("a_qk"), sem("a_ssq"), sem("a_v"), sem("a_k"), sem("a_q")
        a_exp, a_oT, a_onT, a_h2T, a_lsum, a_mask = (sem("a_exp"), sem("a_oT"), sem("a_onT"), sem("a_h2T"),
                                                     sem("a_lsum"), sem("a_mask"))
        v_st1, v_ve1, v_xn, v_ssqe, v_rot, v_rr, v_lo = (sem("v_st1"), sem("v_ve1"), sem("v_xn"), sem("v_ssqe"),
                                                         sem("v_rot"), sem("v_rr"), sem("v_lo"))
        v_pick, v_max, v_sub = sem("v_pick"), sem("v_max"), sem("v_sub")
        v_rden, v_on, v_st2, v_ve2, v_xn2 = sem("v_rden"), sem("v_on"), sem("v_st2"), sem("v_ve2"), sem("v_xn2")
        v_gate, v_onehot, v_psel, v_hm = sem("v_gate"), sem("v_onehot"), sem("v_psel"), sem("v_hm")
        g_rs1, g_rot, g_rqk, g_sel, g_x1, g_rs2 = (sem("g_rs1"), sem("g_rot"), sem("g_rqk"), sem("g_sel"),
                                                   sem("g_x1"), sem("g_rs2"))
        g_yg, g_zg, g_out = sem("g_yg"), sem("g_zg"), sem("g_out")

        W_DMAS = 4

        def scores_of(u):
            b = S_BANK[u]
            return ps[:, b:b + 2, :].rearrange("p b (h t k) -> p (b h) t k", h=2, t=2)

        def slots(x, i, part):
            return x[:, :, part:4:2, :] if i == 0 else x[:, :, 2 * part:2 * part + 2, :]

        def x_of(at):
            b = at.sequence if at.peeled else bass.ds(at.sequence, 1)
            rows = xs[:, b, at.j, :]
            return rows if at.peeled else rows.rearrange("p b d -> p (b d)")

        def heads_twice(x):
            return x.rearrange("p (h d) -> p h d", h=NH).unsqueeze(2).to_broadcast([P, NH, 2, HD])

        block = ctx.enter_context(nc.Block())

        @block.sync
        def _(sp):
            sp.dma_start(c_s[:, :, :], c_t.rearrange("(k p) b -> p k b", p=P)).then_inc(ld_c, 16)
            sp.dma_start(xs[:, 0, 0, :], x_t[0]).then_inc(ld_x[0], 16)
            sp.dma_start(wqkv_s[:, :, :], wqkv.rearrange("(k p) n -> p k n", p=P)).then_inc(ld_wqkv, 16)
            sp.dma_start(xs[:, 0, 1:JT, :], x_t[1:JT].rearrange("j p d -> p j d")).then_inc(ld_x[1], 16)
            sp.dma_start(wo_s[:, :, :], wo.rearrange("(k p) n -> p k n", p=P)).then_inc(ld_w, 16)
            sp.dma_start(gate_s[:, :, :], gate_t.rearrange("(k p) n -> p k n", p=P)).then_inc(ld_w, 16)
            sp.dma_start(up_s[:, :, :], up_t.rearrange("(k p) n -> p k n", p=P)).then_inc(ld_w, 16)
            sp.dma_start(down_s[:, :, :], down.rearrange("(k p) n -> p k n", p=P)).then_inc(ld_w, 16)
            for b in range(1, BATCH):
                sp.dma_start(xs[:, b, :, :], x_t[JT * b:JT * (b + 1)].rearrange("j p d -> p j d")).then_inc(ld_x[2], 16)

            def slot(seq, r, live):
                g = At(seq, r - 3)
                if "G" in live:
                    wait(sp, g_out, g.count(1, 1))
                    sp.dma_start(out_t[g.index], obuf[:, :]).then_inc(st_out, 16)

            run_slots(sp, slot)
            sp.wait_ge(st_out, 16 * TILES)

        @block.tensor
        def _(pe):
            def transposes(dst, srcs, done):
                for i, src in enumerate(srcs):
                    last = pe.transpose(dst[:, i * P:(i + 1) * P], src, ident[:, :])
                last.then_inc(done, 1)

            def project(dst, lhs_t, rhs, parts, done):
                for k in range(parts):
                    last = pe.matmul(dst, lhs_t(k), rhs(k), start=(k == 0), stop=(k == parts - 1))
                last.then_inc(done, 1)

            def modulation(which):
                for i in range(2):
                    for h in range(DC):
                        for k in range(DC):
                            o, m = (i * DC + h) * BATCH, 3 * which + i
                            last = pe.matmul(ps[:, which, o:o + BATCH], wmod_s[:, k, m * D + h * P:m * D + (h + 1) * P],
                                             silu[:, k, :], start=(k == 0), stop=(k == DC - 1))
                last.then_inc(m_cols, 1)

            pe.wait_ge(ld_mod, 16)
            pe.wait_ge(m_silu, 1)
            modulation(0)
            pe.wait_ge(c_ident, 2)

            def gate_rows(b):
                if b == 0:
                    pe.wait_ge(m_silu, 2)
                if b > 1:
                    pe.wait_ge(m_rows_s, b - 1)
                for k in range(DC):
                    last = pe.matmul(ps[:, PT_BANK[b % 2], :], silu_rows[:, k, b, :],
                                     wmod_s[:, k, :].rearrange("p (a m n) -> p a m n", a=2, m=3)[:, :, 2, :],
                                     start=(k == 0), stop=(k == DC - 1))
                last.then_inc(m_rows, 1)

            def scores(t, c):
                u = c % 2
                wait(pe, v_sub, t.count(NC, c - 1))
                wait(pe, a_q, t.count(2, 1 + c // 2))
                wait(pe, a_k, t.count(4, 2 + 2 * (c // 2)))
                if t.peeled and t.index == 0:
                    pe.wait_ge(c_half, 1)
                    pe.wait_ge(m_cols_s, 2)
                for i in range(2):
                    g = 2 * c + i
                    dst = ps[:, S_BANK[u] + i, :].rearrange("p (h n) -> p h n", h=2)
                    if t.j == 0:
                        dst, keys = dst[:, :, P:2 * P], kT[:, g, :, 0, :]
                    else:
                        keys = kT[:, g, :, t.j - 1:t.j + 1, :].rearrange("p h t k -> p h (t k)")
                    last = pe.matmul(dst, qT[:, g, :], keys, start=True, stop=True)
                last.then_inc(p_s, 1)

            def scores_T(t, c):
                wait(pe, a_oT, t.count(NC, c - 1))
                if t.peeled and t.index == 0 and c < 2:
                    pe.wait_ge(m_rows_s, BATCH)
                wait(pe, v_sub, t.count(NC, c + 1))
                transposes(ps[:, PT_BANK[c % 2], :], [shifted[:, c % 2, i, :] for i in range(CH)], p_sT)

            def values(t, c):
                wait(pe, a_v, t.count(1, 1))
                wait(pe, g_sel, t.count(NC, c + 1))
                if t.j > 0:
                    for i in range(CH):
                        pe.matmul(ps[32 * i:32 * i + VW, PT_BANK[c % 2], 0:P], v_s[:, t.j - 1, CH * c + i, :],
                                  prev_p[:, c % 2, i, :], start=True, stop=False)
                for i in range(CH):
                    last = pe.matmul(ps[32 * i:32 * i + VW, PT_BANK[c % 2], 0:P], v_s[:, t.j, CH * c + i, :],
                                     own_p[:, c % 2, i, :], start=(t.j == 0), stop=True)
                last.then_inc(p_pv, 1)

            def qk_T(p, i, n):
                wait(pe, a_hi, p.count(2, 2))
                wait(pe, v_lo, p.count(2, 2))
                srcs = []
                for g in range(CH * n, CH * n + CH):
                    pair = hilo[:, p.k % 2, i, 2 * g:2 * g + 2, :, :].bitcast(F32)
                    srcs.append(pair.rearrange("p h s d -> p (h s d)"))
                transposes(ps[:, W6 if (i, n) == (0, 1) else W7, :], srcs, p_kq)

            def x_T(l):
                wait(pe, v_xn, l.count(1, 1))
                transposes(ps[:, W6, :], [xn[:, k * P:(k + 1) * P] for k in range(DC)], p_xT)

            def queries_keys(x):
                if x.peeled and x.index == 0:
                    pe.wait_ge(ld_wqkv, 16)
                wait(pe, a_hT, x.count(1, 1))
                wait(pe, a_q, x.count(2, -2))
                project(ps[:, W6, :], lambda k: hT[:, k, :], lambda k: wqkv_s[:, k, 0:2 * D], DC, p_qk)

            def values_of(x):
                wait(pe, a_qk, x.count(1, 1))
                project(ps[:, W6, 0:D], lambda k: hT[:, k, :], lambda k: wqkv_s[:, k, 2 * D:3 * D], DC, p_v)

            def slot(seq, r, live):
                l, x, p, t, f, g = (At(seq, r - lag) for lag in range(-2, 4))

                def mask():
                    wait(pe, a_lg, g.count(1, 1))
                    wait(pe, v_onehot, g.count(1, 1))
                    for i in range(EC):
                        chosen = onehot[:, :, :].rearrange("p e r -> p (e r)")[:, i * P:(i + 1) * P]
                        last = pe.matmul(ps[:, W7, i * P:(i + 1) * P], chosen, ident_b[:, :], start=True, stop=True)
                    last.then_inc(p_mask, 1)

                def heads_back():
                    wait(pe, *((a_v, x.count(1, 1)) if "X" in live else
                               (a_q, t.count(2, 2)) if "T" in live else (a_z, g.count(1, 0))))
                    wait(pe, a_oT, f.count(NC, NC))
                    transposes(ps[:, W6, :], [oT[:, i, :] for i in range(NC)], p_o)

                def up():
                    if "T" in live:
                        b = W7
                        wait(pe, a_mask, g.count(1, 1))
                    else:
                        b = S_BANK[0]
                        pe.wait_ge(v_sub, NC * TILES)
                        wait(pe, v_hm, g.count(1, 0))
                    for i in range(EC):
                        for k in range(DC):
                            last = pe.matmul(ps[:, b, i * P:(i + 1) * P], up_s[:, k, i * P:(i + 1) * P],
                                             h2T[:, k, :], start=(k == 0), stop=(k == DC - 1))
                    last.then_inc(p_up, 1)

                def heads_T():
                    wait(pe, v_on, f.count(1, 1))
                    flat = on[:, :, :].rearrange("p h d -> p (h d)")
                    transposes(ps[:, W6, :], [flat[:, k * P:(k + 1) * P] for k in range(DC)], p_onT)

                def project_heads():
                    if f.peeled and f.index == 0:
                        pe.wait_ge(ld_w, 16 * W_DMAS)
                    wait(pe, a_onT, f.count(1, 1))
                    project(ps[:, W6, 0:D], lambda k: onT[:, k, :], lambda k: wo_s[:, k, :], DC, p_wo)

                if "G" in live:
                    wait(pe, *((a_k, t.count(4, 4)) if "T" in live else
                               (v_hm, g.count(1, 0)) if "F" in live else (a_mask, g.count(1, 0))))
                    wait(pe, v_xn2, g.count(1, 1))
                    transposes(ps[:, W7, :], [xn2[:, k * P:(k + 1) * P] for k in range(DC)], p_h2T)
                if "F" in live:
                    values(f, 2)
                if "T" in live:
                    wait(pe, *((a_z, g.count(1, 0)) if not g.peeled or g.index > 0 else (a_hT, x.count(1, 1))))
                    qk_T(t, 0, 1)
                if "F" in live:
                    values(f, 3)
                if "G" in live:
                    wait(pe, a_h2T, g.count(1, 1))
                    project(ps[:, W7, 0:EXPERTS], lambda k: h2T[:, k, :], lambda k: gate_s[:, k, :], DC, p_lg)
                if "X" in live:
                    queries_keys(x)
                if "T" in live:
                    scores_T(t, 0)
                    scores(t, 2)
                    scores_T(t, 1)
                if "X" in live:
                    values_of(x)
                if "G" in live and "T" in live:
                    mask()
                if "T" in live:
                    scores(t, 3)
                if "F" in live:
                    heads_back()
                if "G" in live and "T" in live:
                    up()
                if "F" in live:
                    heads_T()
                if "T" in live:
                    values(t, 0)
                if "P" in live:
                    wait(pe, *((v_hm, g.count(1, 1)) if "G" in live else (a_k, p.count(4, 0))))
                    qk_T(p, 1, 0)
                    if p.peeled and p.index == 0:
                        gate_rows(2)
                if "F" in live:
                    project_heads()
                if "T" in live:
                    values(t, 1)
                if "P" in live:
                    wait(pe, a_k, p.count(4, 2))
                    qk_T(p, 0, 0)
                    if p.peeled and p.index == 0:
                        gate_rows(3)
                if "G" in live and "T" not in live:
                    up()
                    mask()
                if "T" in live:
                    scores_T(t, 2)
                if "L" in live:
                    wait(pe, *((a_y, f.count(1, 1)) if "F" in live else (a_v, x.count(1, 1))))
                    x_T(l)
                if "T" in live:
                    scores_T(t, 3)
                if "P" in live:
                    wait(pe, a_q, p.count(2, 1))
                    qk_T(p, 1, 1)
                    scores(p, 0)
                if "G" in live:
                    wait(pe, *((a_hT, l.count(1, 1)) if "L" in live else
                               (a_y, f.count(1, 1)) if "F" in live else (a_z, g.count(1, 0))))
                    wait(pe, v_hm, g.count(1, 1))
                    project(ps[:, W6, 0:D], lambda k: hm[:, k, :], lambda k: down_s[:, k, :], EC, p_down)
                if "P" in live:
                    scores(p, 1)

            x_T(At(0, 0))
            queries_keys(At(0, 0))
            gate_rows(0)
            values_of(At(0, 0))
            modulation(1)
            gate_rows(1)
            pe.wait_ge(a_v, 1)
            x_T(At(0, 1))
            run_slots(pe, slot)

        @block.scalar
        def _(act):
            target = act.alloc_register("act_target")
            act.dma_start(wmod_s[:, :, :], wmod.rearrange("(k p) n -> p k n", p=P)).then_inc(ld_mod, 16)
            act.dma_start(trig_s[:, :, :, :, :], trig.rearrange("(j p) a b d -> p j a b d", p=P)).then_inc(ld_trig, 16)
            act.dma_start(normw[:, 0, :], qw.partition_broadcast(P)).then_inc(ld_trig, 16)
            act.dma_start(normw[:, 1, :], kw.partition_broadcast(P)).then_inc(ld_trig, 16)
            act.wait_ge(ld_c, 16)
            act.activation(ec[:, :, :], c_s[:, :, :], ACT.Exp, scale=-1.0).then_inc(m_exp, 1)

            def modulation(which):
                act.wait_ge(m_cols, 1 + which)
                act.activation(mod_s[:, 2 * which:2 * which + 2, :, :].rearrange("p m h b -> p (m h b)"),
                               ps[:, which, 0:2 * DC * BATCH], ACT.Identity).then_inc(m_cols_s, 1)

            def gate_rows(b):
                act.wait_ge(m_rows, b + 1)
                act.activation(gates[:, b, :, :].rearrange("p a n -> p (a n)"), ps[:, PT_BANK[b % 2], :],
                               ACT.Identity).then_inc(m_rows_s, 1)

            modulation(0)
            act.wait_ge(m_mod, 1)

            def modulate(dst, b_ps, which, at, done):
                b = at.sequence
                for h in range(DC):
                    last = act.activation(dst[:, h, :], ps[:, b_ps, h * P:(h + 1) * P], ACT.Identity,
                                          scale=mod_s[:, 2 * which + 1, h, bass.ds(b, 1)],
                                          bias=mod_s[:, 2 * which, h, bass.ds(b, 1)])
                last.then_inc(done, 1)

            def hidden(l):
                wait(act, p_v, l.count(1, 0))
                wait_alone(act, p_xT, l.count(1, 1), target, m_mod)
                modulate(hT, W6, 0, l, a_hT)

            def queries_keys(x):
                wait(act, g_rot, x.count(3, 0))
                wait(act, a_ssq, x.count(2, 0))
                wait(act, p_qk, x.count(1, 1))
                act.activation(qk[:, :, :].rearrange("p a d -> p (a d)"), ps[:, W6, :],
                               ACT.Identity).then_inc(a_qk, 1)

            def squares(x, i):
                if i == 0:
                    wait(act, a_qk, x.count(1, 1))
                    wait(act, v_ssqe, x.count(1, 0))
                wait(act, a_ssq, x.count(2, i))
                act.activation(sq[:, :], qk[:, i, :], ACT.Square, accum_out=ssq[:, i:i + 1]).then_inc(a_ssq, 1)

            def high(x, i):
                wait(act, p_kq, x.count(4, -4))
                wait(act, g_rqk, x.count(1, 1))
                wait(act, v_rot, x.count(1, 1))
                act.activation(slots(hilo[:, x.k % 2, i, :, :, :], i, 0), heads_twice(rot[:, i, :]), ACT.Identity,
                               scale=rqk[:, i:i + 1]).then_inc(a_hi, 1)

            def values_of(x):
                wait(act, p_pv, x.count(NC, -2 * NC))
                if x.peeled and x.index == 0:
                    act.wait_ge(c_ones, 1)
                wait(act, p_v, x.count(1, 1))
                act.activation(v_s[:, x.j, :, 0:HD], ps[:, W6, 0:D].rearrange("p (h d) -> p h d", h=NH),
                               ACT.Identity).then_inc(a_v, 1)

            def slot(seq, r, live):
                l, x, p, t, f, g = (At(seq, r - lag) for lag in range(-2, 4))

                def exps(c):
                    wait(act, g_sel, t.count(NC, c - 1))
                    wait(act, p_sT, t.count(NC, c + 1))
                    act.activation(expT[:, c % 2, :, :].rearrange("p h q -> p (h q)"), ps[:, PT_BANK[c % 2], :],
                                   ACT.Exp).then_inc(a_exp, 1)

                def out_T(t, c):
                    wait(act, p_o, t.count(1, 0))
                    wait(act, p_pv, t.count(NC, c + 1))
                    act.activation(oT[:, c, :], ps[:, PT_BANK[c % 2], 0:P], ACT.Identity).then_inc(a_oT, 1)

                def k_rows(n):
                    wait(act, p_s, p.count(NC, -2 * NC))
                    wait(act, p_kq, p.count(4, 2 * n + 1))
                    for h in range(2):
                        act.activation(kT[64 * h:64 * h + 64, CH * n:CH * n + CH, h, p.j, :],
                                       ps[64 * h:64 * h + 64, W7, :].rearrange("p (g k) -> p g k", g=CH),
                                       ACT.Identity).then_inc(a_k, 1)

                def q_rows(p, n):
                    wait(act, p_s, p.count(NC, 0))
                    wait(act, p_kq, p.count(4, 2 * n + 2))
                    act.activation(qT[:, CH * n:CH * n + CH, :].rearrange("p g k -> p (g k)"), ps[:, W6 if n else W7, :],
                                   ACT.Identity).then_inc(a_q, 1)

                def sums():
                    wait(act, v_psel, g.count(1, 0))
                    wait(act, v_gate, g.count(4, 1))
                    act.activation(lexp[:, :], lgs[:, :], ACT.Exp, bias=nmx[:, :], accum_out=lsum[:, :]).then_inc(a_lsum, 1)

                def mask():
                    wait(act, v_hm, g.count(1, 0))
                    wait(act, p_mask, g.count(1, 1))
                    act.activation(maskT[:, :, :].rearrange("p e t -> p (e t)"), ps[:, W7, :],
                                   ACT.Identity).then_inc(a_mask, 1)

                if "G" in live:
                    if g.peeled and g.index == 0:
                        act.wait_ge(m_mod, 2)
                    wait(act, p_up, g.count(1, 0))
                    wait_alone(act, p_h2T, g.count(1, 1), target, m_mod)
                    modulate(h2T, W7, 1, g, a_h2T)
                if "F" in live:
                    out_T(f, 2)
                if "T" in live:
                    q_rows(t, 1)
                if "P" in live:
                    high(p, 0)
                if "F" in live:
                    out_T(f, 3)
                if "G" in live:
                    wait(act, v_onehot, g.count(1, 0))
                    wait(act, p_lg, g.count(1, 1))
                    act.activation(lgs[:, :], ps[:, W7, 0:EXPERTS], ACT.Identity).then_inc(a_lg, 1)
                if "G" in live and "T" in live:
                    sums()
                if "X" in live:
                    queries_keys(x)
                if "T" in live:
                    exps(0)
                    exps(1)
                if "X" in live:
                    values_of(x)
                if "G" in live and "T" in live:
                    mask()
                if "X" in live:
                    squares(x, 0)
                if "F" in live:
                    wait(act, p_wo, f.count(1, 0))
                    wait(act, p_onT, f.count(1, 1))
                    act.activation(onT[:, :, :].rearrange("p k t -> p (k t)"), ps[:, W6, 0:D],
                                   ACT.Identity).then_inc(a_onT, 1)
                if "X" in live:
                    squares(x, 1)
                if "T" in live:
                    out_T(t, 0)
                if "P" in live:
                    k_rows(0)
                    if p.peeled and p.index == 0:
                        gate_rows(2)
                if "F" in live:
                    wait(act, g_yg, f.count(1, 0))
                    wait(act, p_wo, f.count(1, 1))
                    act.activation(y[:, :], ps[:, W6, 0:D], ACT.Identity).then_inc(a_y, 1)
                if "T" in live:
                    out_T(t, 1)
                if "G" in live and "T" not in live:
                    sums()
                    mask()
                if "P" in live:
                    q_rows(p, 0)
                    if p.peeled and p.index == 0:
                        gate_rows(3)
                if "T" in live:
                    exps(2)
                if "L" in live:
                    hidden(l)
                if "T" in live:
                    exps(3)
                if "P" in live:
                    k_rows(1)
                if "X" in live:
                    high(x, 1)
                if "G" in live:
                    wait(act, g_zg, g.count(1, 0))
                    wait(act, v_psel, g.count(1, 1))
                    wait(act, p_down, g.count(1, 1))
                    act.activation(z[:, :], ps[:, W6, 0:D], ACT.Identity, scale=psel[:, :]).then_inc(a_z, 1)

            hidden(At(0, 0))
            queries_keys(At(0, 0))
            squares(At(0, 0), 0)
            squares(At(0, 0), 1)
            gate_rows(0)
            values_of(At(0, 0))
            modulation(1)
            gate_rows(1)
            hidden(At(0, 1))
            high(At(0, 0), 1)
            run_slots(act, slot)

        @block.vector
        def _(dve):
            target = dve.alloc_register("dve_target")
            dve.memset(kT[0:64, :, 1, :, :].bitcast(F32), 0.0).then_inc(c_zero, 1)
            dve.wait_ge(m_exp, 1)
            dve.tensor_scalar(ec1[:, :, :], ec[:, :, :], 1.0, None, ALU.add).then_inc(m_dve, 1)
            dve.wait_ge(m_dve, 1)
            dve.reciprocal(sig[:, :, :], ec1[:, :, :]).then_inc(m_dve, 1)
            dve.wait_ge(m_dve, 2)
            dve.tensor_tensor(silu[:, :, :], c_s[:, :, :], sig[:, :, :], ALU.mult).then_inc(m_silu, 1)
            dve.wait_ge(m_silu, 1)
            dve.tensor_copy(silu_rows[:, :, :, :], silu[:, :, :].unsqueeze(3).to_broadcast([P, DC, BATCH, P])).then_inc(m_silu, 1)

            def sums(src, st, s_st, at):
                dve.bn_stats(out=st[:, :], in_=src).then_inc(s_st, 1)

            def variance(st, mv, ve, s_st, s_ve, at):
                wait_alone(dve, s_st, at.count(2, 1), target, c_zero)
                dve.bn_aggr(out=mv[:, :], in_=st[:, :]).then_inc(s_st, 1)
                wait(dve, s_st, at.count(2, 2))
                dve.tensor_scalar(ve[:, :], mv[:, 1:2], EPS_LN, None, ALU.add).then_inc(s_ve, 1)

            def normed(dst, src, mv, rs, done):
                dve.tensor_scalar(dst[:, :], src, mv[:, 0:1], rs[:, 0:1], ALU.subtract, ALU.mult).then_inc(done, 1)

            def ln1_sums(at):
                if at.peeled and at.index in (0, 1, JT):
                    part = (0, 1, JT).index(at.index)
                    dve.wait_ge(ld_x[part], 16 if part < 2 else 16 * (BATCH - 1))
                wait(dve, g_rs1, at.count(1, 0))
                sums(x_of(at), st1, v_st1, at)

            def ln1_variance(at):
                variance(st1, mv1, ve1, v_st1, v_ve1, at)

            def ln1(at):
                wait(dve, p_xT, at.count(1, 0))
                wait(dve, g_rs1, at.count(1, 1))
                normed(xn, x_of(at), mv1, rs1, v_xn)

            ln1_sums(At(0, 0))
            ln1_variance(At(0, 0))
            dve.wait_ge(c_pool, 1)
            dve.tensor_copy(take_prev[:, :], take_f[:, :]).then_inc(c_pick, 1)
            dve.wait_ge(m_cols_s, 1)
            dve.tensor_scalar(mod_s[:, 1, :, :], mod_s[:, 1, :, :], 1.0, None, ALU.add).then_inc(m_mod, 1)
            ln1(At(0, 0))
            dve.wait_ge(ld_trig, 48)
            for i in range(2):
                w = normw[:, i, :].rearrange("p (h d) -> p h d", h=NH)
                dve.tensor_tensor(cosw[:, :, i, :].rearrange("p j (h d) -> p j h d", h=NH),
                                  w.unsqueeze(1).to_broadcast([P, JT, NH, HD]),
                                  trig_s[:, :, i, 0, :].unsqueeze(2).to_broadcast([P, JT, NH, HD]),
                                  ALU.mult).then_inc(c_rope, 1)
                for a in range(2):
                    dve.tensor_tensor(
                        sinw[:, :, i, :].rearrange("p j (h a d) -> p j h a d", h=NH, a=2)[:, :, :, a, :],
                        w[:, :, HALF * (1 - a):HALF * (2 - a)].unsqueeze(1).to_broadcast([P, JT, NH, HALF]),
                        trig_s[:, :, i, 1, HALF * a:HALF * (a + 1)].unsqueeze(2).to_broadcast([P, JT, NH, HALF]),
                        ALU.mult).then_inc(c_rope, 1)

            def mean_squares(x):
                wait(dve, g_rqk, x.count(1, 0))
                wait(dve, a_ssq, x.count(2, 2))
                dve.tensor_scalar(ssqe[:, :], ssq[:, :], 1.0 / D, EPS_RMS, ALU.mult, ALU.add).then_inc(v_ssqe, 1)

            def rotated(x):
                flat = [x.rearrange("p a d -> p (a d)") for x in (rot[:, :, :], t1[:, :, :], t2[:, :, :])]
                wait(dve, a_hi, x.count(2, 0))
                wait(dve, g_rot, x.count(3, 3))
                dve.tensor_tensor(*flat, ALU.add).then_inc(v_rot, 1)

            def scaled(x):
                wait(dve, v_rot, x.count(1, 1))
                wait(dve, g_rqk, x.count(1, 1))
                for i in range(2):
                    dve.tensor_scalar(rr[:, i, :], rot[:, i, :], rqk[:, i:i + 1], None, ALU.mult).then_inc(v_rr, 1)

            def gate_values(b):
                raw = gates[:, b, :, :].rearrange("p a n -> p (a n)")
                dve.wait_ge(m_rows_s, b + 1)
                if b:
                    dve.wait_ge(m_gates, b)
                dve.tensor_scalar(gsgn[:, :], raw, 0.0, 2.0, ALU.is_ge, ALU.mult).then_inc(m_gdve, 1)
                dve.scalar_tensor_tensor(out=gtmp[:, :], in0=raw, scalar=-1.0, in1=raw, op0=ALU.mult,
                                         op1=ALU.max).then_inc(m_gdve, 1)
                dve.wait_ge(m_gdve, 4 * b + 2)
                dve.tensor_scalar(gtmp[:, 0:D], gtmp[:, 0:D], 0.25, None, ALU.max).then_inc(m_gdve, 1)
                dve.tensor_scalar(gtmp[:, D:2 * D], gtmp[:, D:2 * D], 0.25, SCALING, ALU.max,
                                  ALU.mult).then_inc(m_gdve, 1)
                dve.wait_ge(m_gdve, 4 * b + 4)
                dve.scalar_tensor_tensor(out=raw, in0=gsgn[:, :], scalar=-1.0, in1=gtmp[:, :], op0=ALU.add,
                                         op1=ALU.mult).then_inc(m_gates, 1)

            def slot(seq, r, live):
                l, x, p, t, f, g = (At(seq, r - lag) for lag in range(-2, 4))

                def own(c):
                    return scores_of(c % 2)[:, :, 1, :]

                def merge(c):
                    pick = take_prev[:, :].unsqueeze(1).to_broadcast([P, CH, P])
                    other = (scores_of(c % 2)[:, :, 0, :] if t.j else
                             neg_s[:, :].unsqueeze(1).to_broadcast([P, CH, P]))
                    if t.peeled and t.index == 0:
                        dve.wait_ge(c_pick, 1)
                        dve.wait_ge(c_ones, 1)
                    wait_alone(dve, p_s, t.count(NC, c + 1), target, c_zero)
                    dve.copy_predicated(own(c), pick, other).then_inc(v_pick, 1)

                def maximum(c):
                    wait(dve, v_pick, t.count(NC, c + 1))
                    dve.tensor_reduce(negm[:, c % 2, :], own(c), AX.X, ALU.max, negate=True).then_inc(v_max, 1)

                def subtract(c):
                    wait(dve, p_sT, t.count(NC, c - 1))
                    wait(dve, v_max, t.count(NC, c + 1))
                    dve.tensor_tensor(shifted[:, c % 2, :, :], own(c),
                                      negm[:, c % 2, :].unsqueeze(2).to_broadcast([P, CH, P]),
                                      ALU.add).then_inc(v_sub, 1)

                def lo(i, n):
                    if n == 0:
                        wait(dve, v_rr, p.count(2, 2))
                        wait(dve, p_kq, p.count(4, -4))
                    wait(dve, a_hi, p.count(2, 1 + n))
                    dve.tensor_tensor(slots(hilo[:, p.k % 2, i, :, :, :], i, 1), heads_twice(rr[:, i, :]),
                                      slots(hilo[:, p.k % 2, i, :, :, :], i, 0).bitcast(F32), ALU.subtract).then_inc(v_lo, 1)

                def first_expert():
                    wait(dve, a_lsum, g.count(1, 0))
                    wait(dve, a_lg, g.count(1, 1))
                    dve.tensor_reduce(nmx[:, :], lgs[:, :], AX.X, ALU.max, negate=True).then_inc(v_gate, 1)

                def count_down():
                    wait(dve, v_gate, g.count(4, 1))
                    dve.tensor_scalar(ge[:, :], lgs[:, :], nmx[:, :], 0.0, ALU.add, ALU.is_ge).then_inc(v_gate, 1)
                    wait(dve, v_gate, g.count(4, 2))
                    dve.tensor_tensor(score[:, :], ge[:, :], first_s[:, :], ALU.mult).then_inc(v_gate, 1)

                def choose():
                    wait(dve, v_gate, g.count(4, 3))
                    dve.tensor_reduce(best[:, :], score[:, :], AX.X, ALU.max).then_inc(v_gate, 1)
                    wait(dve, p_mask, g.count(1, 0))
                    wait(dve, v_gate, g.count(4, 4))
                    dve.tensor_scalar(onehot[:, :, :], score[:, :].unsqueeze(2).to_broadcast([P, EXPERTS, RANK]),
                                      best[:, :], None, ALU.is_equal).then_inc(v_onehot, 1)

                def probability():
                    wait(dve, a_z, g.count(1, 0))
                    wait(dve, a_lsum, g.count(1, 1))
                    dve.reciprocal(psel[:, :], lsum[:, :]).then_inc(v_psel, 1)

                def hidden_rows():
                    wait(dve, a_mask, g.count(1, 1))
                    wait(dve, p_down, g.count(1, 0))
                    wait(dve, p_up, g.count(1, 1))
                    dve.tensor_tensor(hm[:, :, :].rearrange("p e t -> p (e t)"), ps[:, W7 if "T" in live else S_BANK[0], :],
                                      maskT[:, :, :].rearrange("p e t -> p (e t)"), ALU.mult).then_inc(v_hm, 1)

                if "T" in live:
                    merge(0)
                if "G" in live:
                    wait(dve, p_h2T, g.count(1, 0))
                    wait(dve, g_rs2, g.count(1, 1))
                    normed(xn2, x1[:, g.k % 2, :], mv2, rs2, v_xn2)
                if "T" in live:
                    maximum(0)
                    merge(1)
                    maximum(1)
                    subtract(0)
                if "P" in live:
                    lo(1, 0)
                if "G" in live and "T" in live:
                    first_expert()
                if "T" in live:
                    subtract(1)
                if "G" in live and "T" in live:
                    count_down()
                if "L" in live:
                    ln1_sums(l)
                if "G" in live and "T" in live:
                    choose()
                if "P" in live:
                    lo(0, 1)
                if "L" in live:
                    ln1_variance(l)
                if "G" in live and "T" in live:
                    probability()
                if "T" in live:
                    merge(2)
                    merge(3)
                if "F" in live:
                    heads = ps[:, W6, :].rearrange("p (h d) -> p h d", h=NH)
                    wait(dve, p_o, f.count(1, 1))
                    dve.reciprocal(rden[:, :], heads[:, :, HD]).then_inc(v_rden, 1)
                    wait(dve, v_rden, f.count(1, 1))
                    wait(dve, p_onT, f.count(1, 0))
                    dve.tensor_tensor(on[:, :, :], heads[:, :, 0:HD],
                                      rden[:, :].unsqueeze(2).to_broadcast([P, NH, HD]), ALU.mult).then_inc(v_on, 1)
                if "G" in live and "T" not in live:
                    first_expert()
                    count_down()
                    choose()
                    probability()
                if "G" in live and "T" in live:
                    hidden_rows()
                if "T" in live:
                    maximum(2)
                if "L" in live:
                    ln1(l)
                if "X" in live:
                    mean_squares(x)
                if "T" in live:
                    maximum(3)
                    subtract(2)
                    subtract(3)
                if "X" in live:
                    rotated(x)
                    scaled(x)
                if "G" in live and "T" not in live:
                    hidden_rows()
                if p.peeled and p.index == 0:
                    dve.wait_ge(m_cols_s, 2)
                    dve.tensor_scalar(mod_s[:, 3, :, :], mod_s[:, 3, :, :], 1.0, None, ALU.add).then_inc(m_mod, 1)
                if "F" in live:
                    wait(dve, g_rs2, f.count(1, 0))
                    wait(dve, g_x1, f.count(1, 1))
                    sums(x1[:, f.k % 2, :], st2, v_st2, f)
                if p.peeled and p.index < BATCH:
                    gate_values(p.index)
                if "F" in live:
                    variance(st2, mv2, ve2, v_st2, v_ve2, f)

            ln1_sums(At(0, 1))
            ln1_variance(At(0, 1))
            ln1(At(0, 1))
            mean_squares(At(0, 0))
            rotated(At(0, 0))
            scaled(At(0, 0))
            run_slots(dve, slot)

        @block.gpsimd
        def _(pool):
            target = pool.alloc_register("pool_target")
            pool.memset(ones_f[:, :], 1.0).then_inc(c_const, 1)
            pool.memset(pow_s[:, :], -0.5).then_inc(c_const, 1)
            pool.wait_ge(c_const, 2)
            pool.affine_select(out=ident[:, :], in_=ones_f[:, :], compare_op=ALU.is_equal, fill=0.0, base=0,
                               pattern=[[1, P]], channel_multiplier=-1).then_inc(c_ident, 1)
            pool.affine_select(out=ident_b[:, :], in_=ones_f[:, :], compare_op=ALU.is_equal, fill=0.0, base=0,
                               pattern=[[1, P]], channel_multiplier=-1).then_inc(c_ident, 1)
            pool.affine_select(out=take_f[:, :], in_=ones_f[:, :], compare_op=ALU.is_ge, fill=0.0, base=-1,
                               pattern=[[1, P]], channel_multiplier=-1).then_inc(c_pool, 1)
            pool.wait_ge(v_ve1, 1)
            pool.tensor_tensor(rs1[:, :], ve1[:, :], pow_s[:, 0:1], ALU.pow).then_inc(g_rs1, 1)
            pool.memset(neg_s[:, :], NEG)
            for e in range(EXPERTS):
                pool.memset(first_s[:, e:e + 1], float(EXPERTS - e))
            pool.memset(v_s[:, :, :, HD:VW], 1.0).then_inc(c_ones, 1)
            pool.wait_ge(c_ones, 1)
            pool.memset(kT[64:128, :, 0, :, :].bitcast(F32), 0.0).then_inc(c_half, 1)
            pool.wait_ge(c_half, 1)

            def rotate(x):
                wait(pool, v_rot, x.count(1, 0))
                if x.peeled and x.index == 0:
                    pool.wait_ge(c_rope, 6)
                wait(pool, a_qk, x.count(1, 1))
                pool.tensor_tensor(t1[:, :, :], qk[:, :, :], cosw[:, x.j, :, :], ALU.mult).then_inc(g_rot, 1)
                halves = [x.rearrange("p i (h a d) -> p (i h) a d", h=NH, a=2)
                          for x in (t2[:, :, :], qk[:, :, :], sinw[:, x.j, :, :])]
                for a in range(2):
                    pool.tensor_tensor(halves[0][:, :, a, :], halves[1][:, :, 1 - a, :], halves[2][:, :, a, :],
                                       ALU.mult).then_inc(g_rot, 1)

            def inverse_rms(x):
                wait(pool, v_rr, x.count(2, 0))
                wait(pool, a_hi, x.count(2, 0))
                wait(pool, v_ssqe, x.count(1, 1))
                pool.tensor_tensor(rqk[:, :], ssqe[:, :], pow_s[:, :], ALU.pow).then_inc(g_rqk, 1)

            def slot(seq, r, live):
                l, x, p, t, f, g = (At(seq, r - lag) for lag in range(-2, 4))

                def select(t, c):
                    u = c % 2
                    wait_alone(pool, a_exp, t.count(NC, c + 1), target, c_const)
                    if t.j:
                        pool.affine_select(out=prev_p[:, u, :, :], in_=expT[:, u, :, :], compare_op=ALU.is_ge,
                                           fill=0.0, base=-1, pattern=[[0, CH], [-1, P]], channel_multiplier=1)
                    pool.affine_select(out=own_p[:, u, :, :], in_=expT[:, u, :, :], compare_op=ALU.is_ge,
                                       fill=0.0, base=0, pattern=[[0, CH], [1, P]],
                                       channel_multiplier=-1).then_inc(g_sel, 1)

                if "T" in live:
                    select(t, 0)
                    select(t, 1)
                if "L" in live:
                    wait(pool, v_xn, l.count(1, 0))
                    wait(pool, v_ve1, l.count(1, 1))
                    pool.tensor_tensor(rs1[:, :], ve1[:, :], pow_s[:, 0:1], ALU.pow).then_inc(g_rs1, 1)
                if "X" in live:
                    rotate(x)
                    inverse_rms(x)
                if "F" in live:
                    if f.peeled and f.index == 0:
                        pool.wait_ge(m_gates, 1)
                    wait_alone(pool, a_y, f.count(1, 1), target, c_const)
                    pool.tensor_tensor(yg[:, :], y[:, :], gates[:, f.sequence, 0, :], ALU.mult).then_inc(g_yg, 1)
                    wait(pool, g_out, f.count(1, -1))
                    wait(pool, g_yg, f.count(1, 1))
                    pool.tensor_tensor(x1[:, f.k % 2, :], x_of(f), yg[:, :], ALU.add).then_inc(g_x1, 1)
                if "T" in live:
                    select(t, 2)
                if "F" in live:
                    wait(pool, v_xn2, f.count(1, 0))
                    wait(pool, v_ve2, f.count(1, 1))
                    pool.tensor_tensor(rs2[:, :], ve2[:, :], pow_s[:, 0:1], ALU.pow).then_inc(g_rs2, 1)
                if "T" in live:
                    select(t, 3)
                if "G" in live:
                    if "F" not in live:
                        pool.wait_ge(g_out, TILES - 1)
                    wait_alone(pool, a_z, g.count(1, 1), target, c_const)
                    pool.tensor_tensor(zg[:, :], z[:, :], gates[:, g.sequence, 1, :], ALU.mult).then_inc(g_zg, 1)
                    wait(pool, st_out, g.count(16, 0))
                    wait(pool, g_zg, g.count(1, 1))
                    pool.tensor_tensor(obuf[:, :], x1[:, g.k % 2, :], zg[:, :], ALU.add).then_inc(g_out, 1)

                if p.peeled and p.index == BATCH - 1:
                    pool.wait_ge(m_gates, BATCH)

            pool.wait_ge(v_xn, 1)
            pool.wait_ge(v_ve1, 2)
            pool.tensor_tensor(rs1[:, :], ve1[:, :], pow_s[:, 0:1], ALU.pow).then_inc(g_rs1, 1)
            rotate(At(0, 0))
            inverse_rms(At(0, 0))
            run_slots(pool, slot)


def rotation_tables():
    inv = (1.0 / np.float32(10000.0) ** (np.arange(0, HD, 2, dtype=np.float32) / np.float32(HD))).astype(np.float32)
    angle = np.arange(SEQ, dtype=np.float32)[:, None] * inv[None, :]
    cos, sin = np.cos(angle).astype(np.float32), np.sin(angle).astype(np.float32)
    k = np.stack([np.concatenate([cos, cos], 1), np.concatenate([-sin, sin], 1)], 1)
    return np.ascontiguousarray(np.stack([k * np.float32(HD ** -0.5), k], 1))


def kernel(L0_attn_hidden_states, L0_attn_Wqkv, L0_attn_q_norm_w, L0_attn_k_norm_w, L0_attn_Wo, L0_ffn_A,
           L0_ffn_Bw, L0_ffn_Wg, L0_c, L0_wmod):
    import concourse.bacc as bacc
    from concourse.bass_utils import run_bass_kernel_spmd

    arrays = {
        "x": np.asarray(L0_attn_hidden_states).reshape(BATCH * SEQ, D),
        "c_t": np.asarray(L0_c).T,
        "wmod": np.asarray(L0_wmod),
        "wqkv": np.asarray(L0_attn_Wqkv),
        "qw": np.asarray(L0_attn_q_norm_w),
        "kw": np.asarray(L0_attn_k_norm_w),
        "wo": np.asarray(L0_attn_Wo),
        "up_t": np.asarray(L0_ffn_A).reshape(ER, D).T,
        "down": np.asarray(L0_ffn_Bw).transpose(0, 2, 1).reshape(ER, D),
        "gate_t": np.asarray(L0_ffn_Wg).T,
        "trig": rotation_tables(),
    }
    arrays = {n: np.ascontiguousarray(a) for n, a in arrays.items()}
    nc = bacc.Bacc("TRN2", target_bir_lowering=False, num_devices=1)
    ins = [nc.dram_tensor(n, a.shape, mybir.dt.from_np(a.dtype), kind="ExternalInput").ap() for n, a in arrays.items()]
    out = nc.dram_tensor("out", (BATCH * SEQ, D), F32, kind="ExternalOutput").ap()
    build(nc, *ins, out)
    r = run_bass_kernel_spmd(nc, [arrays], core_ids=[0])
    return r.results[0]["out"].reshape(BATCH, SEQ, D)
```
